# Optimizing a Trainium2 kernel written in Bass

```python
import numpy as np
import jax
import jax.numpy as jnp

def _softmax(x, axis=-1):
    return jax.nn.softmax(x, axis=axis)

def _gelu(x):
    return jax.nn.gelu(x, approximate=True)

def _silu(x):
    return jax.nn.silu(x)

def _sigmoid(x):
    return jax.nn.sigmoid(x)

def _layernorm(x, axis=-1, eps=1e-05):
    m = jnp.mean(x, axis=axis, keepdims=True)
    v = jnp.var(x, axis=axis, keepdims=True)
    return (x - m) / jnp.sqrt(v + eps)

def _scatter_add(tgt, idx, src, axis=0):
    return tgt.at[idx].add(src)

def _segment_sum(src, seg, n):
    return jax.ops.segment_sum(src, seg, n)
kernel_name = 'mk_dlrm_tower_d1_rec_r8_5aebca'

def setup_inputs(seed: int=0):
    np.random.seed(seed)
    _w = jnp.asarray

    def _rec_inputs():
        import jax
        import jax.numpy as jnp
        _tk = jax.random.key(seed)
        dense_ctx = jax.random.normal(jax.random.fold_in(_tk, 190), (2048, 16), jnp.float32)
        ids = jnp.stack([jax.random.randint(jax.random.fold_in(_tk, 200 + f), (2048,), 0, v, jnp.int32) for f, v in enumerate([1250, 1250, 125000, 125000, 12500, 125000, 125000, 125000, 1250, 12500, 12500, 12500, 12500, 12500, 1000, 1000, 125000, 12500, 1000, 1000, 1250, 12500, 1250, 12500, 12500, 1250, 125000, 125000, 1250, 1250, 12500, 12500, 12500, 125000, 125000, 1250, 125000, 1250, 1250])], axis=1)
        tbl_0 = 0.05 * jax.random.normal(jax.random.fold_in(_tk, 500 + 0), (1250, 16), jnp.float32)
        tbl_1 = 0.05 * jax.random.normal(jax.random.fold_in(_tk, 500 + 1), (1250, 16), jnp.float32)
        tbl_2 = 0.05 * jax.random.normal(jax.random.fold_in(_tk, 500 + 2), (125000, 16), jnp.float32)
        tbl_3 = 0.05 * jax.random.normal(jax.random.fold_in(_tk, 500 + 3), (125000, 16), jnp.float32)
        tbl_4 = 0.05 * jax.random.normal(jax.random.fold_in(_tk, 500 + 4), (12500, 16), jnp.float32)
        tbl_5 = 0.05 * jax.random.normal(jax.random.fold_in(_tk, 500 + 5), (125000, 16), jnp.float32)
        tbl_6 = 0.05 * jax.random.normal(jax.random.fold_in(_tk, 500 + 6), (125000, 16), jnp.float32)
        tbl_7 = 0.05 * jax.random.normal(jax.random.fold_in(_tk, 500 + 7), (125000, 16), jnp.float32)
        tbl_8 = 0.05 * jax.random.normal(jax.random.fold_in(_tk, 500 + 8), (1250, 16), jnp.float32)
        tbl_9 = 0.05 * jax.random.normal(jax.random.fold_in(_tk, 500 + 9), (12500, 16), jnp.float32)
        tbl_10 = 0.05 * jax.random.normal(jax.random.fold_in(_tk, 500 + 10), (12500, 16), jnp.float32)
        tbl_11 = 0.05 * jax.random.normal(jax.random.fold_in(_tk, 500 + 11), (12500, 16), jnp.float32)
        tbl_12 = 0.05 * jax.random.normal(jax.random.fold_in(_tk, 500 + 12), (12500, 16), jnp.float32)
        tbl_13 = 0.05 * jax.random.normal(jax.random.fold_in(_tk, 500 + 13), (12500, 16), jnp.float32)
        tbl_14 = 0.05 * jax.random.normal(jax.random.fold_in(_tk, 500 + 14), (1000, 16), jnp.float32)
        tbl_15 = 0.05 * jax.random.normal(jax.random.fold_in(_tk, 500 + 15), (1000, 16), jnp.float32)
        tbl_16 = 0.05 * jax.random.normal(jax.random.fold_in(_tk, 500 + 16), (125000, 16), jnp.float32)
        tbl_17 = 0.05 * jax.random.normal(jax.random.fold_in(_tk, 500 + 17), (12500, 16), jnp.float32)
        tbl_18 = 0.05 * jax.random.normal(jax.random.fold_in(_tk, 500 + 18), (1000, 16), jnp.float32)
        tbl_19 = 0.05 * jax.random.normal(jax.random.fold_in(_tk, 500 + 19), (1000, 16), jnp.float32)
        tbl_20 = 0.05 * jax.random.normal(jax.random.fold_in(_tk, 500 + 20), (1250, 16), jnp.float32)
        tbl_21 = 0.05 * jax.random.normal(jax.random.fold_in(_tk, 500 + 21), (12500, 16), jnp.float32)
        tbl_22 = 0.05 * jax.random.normal(jax.random.fold_in(_tk, 500 + 22), (1250, 16), jnp.float32)
        tbl_23 = 0.05 * jax.random.normal(jax.random.fold_in(_tk, 500 + 23), (12500, 16), jnp.float32)
        tbl_24 = 0.05 * jax.random.normal(jax.random.fold_in(_tk, 500 + 24), (12500, 16), jnp.float32)
        tbl_25 = 0.05 * jax.random.normal(jax.random.fold_in(_tk, 500 + 25), (1250, 16), jnp.float32)
        tbl_26 = 0.05 * jax.random.normal(jax.random.fold_in(_tk, 500 + 26), (125000, 16), jnp.float32)
        tbl_27 = 0.05 * jax.random.normal(jax.random.fold_in(_tk, 500 + 27), (125000, 16), jnp.float32)
        tbl_28 = 0.05 * jax.random.normal(jax.random.fold_in(_tk, 500 + 28), (1250, 16), jnp.float32)
        tbl_29 = 0.05 * jax.random.normal(jax.random.fold_in(_tk, 500 + 29), (1250, 16), jnp.float32)
        tbl_30 = 0.05 * jax.random.normal(jax.random.fold_in(_tk, 500 + 30), (12500, 16), jnp.float32)
        tbl_31 = 0.05 * jax.random.normal(jax.random.fold_in(_tk, 500 + 31), (12500, 16), jnp.float32)
        tbl_32 = 0.05 * jax.random.normal(jax.random.fold_in(_tk, 500 + 32), (12500, 16), jnp.float32)
        tbl_33 = 0.05 * jax.random.normal(jax.random.fold_in(_tk, 500 + 33), (125000, 16), jnp.float32)
        tbl_34 = 0.05 * jax.random.normal(jax.random.fold_in(_tk, 500 + 34), (125000, 16), jnp.float32)
        tbl_35 = 0.05 * jax.random.normal(jax.random.fold_in(_tk, 500 + 35), (1250, 16), jnp.float32)
        tbl_36 = 0.05 * jax.random.normal(jax.random.fold_in(_tk, 500 + 36), (125000, 16), jnp.float32)
        tbl_37 = 0.05 * jax.random.normal(jax.random.fold_in(_tk, 500 + 37), (1250, 16), jnp.float32)
        tbl_38 = 0.05 * jax.random.normal(jax.random.fold_in(_tk, 500 + 38), (1250, 16), jnp.float32)
        _rk = jax.random.fold_in(_tk, 7)
        W_top1 = 0.0606339 * jax.random.normal(jax.random.fold_in(_tk, 801), (272, 512), jnp.float32)
        W_top2 = 0.0441942 * jax.random.normal(jax.random.fold_in(_tk, 802), (512, 256), jnp.float32)
        W_top3 = 0.0625 * jax.random.normal(jax.random.fold_in(_tk, 803), (256, 1), jnp.float32)
        b_top1 = jnp.zeros((512,), jnp.float32)
        b_top2 = jnp.zeros((256,), jnp.float32)
        return (dense_ctx, ids, tbl_0, tbl_1, tbl_2, tbl_3, tbl_4, tbl_5, tbl_6, tbl_7, tbl_8, tbl_9, tbl_10, tbl_11, tbl_12, tbl_13, tbl_14, tbl_15, tbl_16, tbl_17, tbl_18, tbl_19, tbl_20, tbl_21, tbl_22, tbl_23, tbl_24, tbl_25, tbl_26, tbl_27, tbl_28, tbl_29, tbl_30, tbl_31, tbl_32, tbl_33, tbl_34, tbl_35, tbl_36, tbl_37, tbl_38, W_top1, b_top1, W_top2, b_top2, W_top3)
    dense_ctx, ids, tbl_0, tbl_1, tbl_2, tbl_3, tbl_4, tbl_5, tbl_6, tbl_7, tbl_8, tbl_9, tbl_10, tbl_11, tbl_12, tbl_13, tbl_14, tbl_15, tbl_16, tbl_17, tbl_18, tbl_19, tbl_20, tbl_21, tbl_22, tbl_23, tbl_24, tbl_25, tbl_26, tbl_27, tbl_28, tbl_29, tbl_30, tbl_31, tbl_32, tbl_33, tbl_34, tbl_35, tbl_36, tbl_37, tbl_38, W_top1, b_top1, W_top2, b_top2, W_top3 = _rec_inputs()

    def _L0_rec_setup():
        import jax, jax.numpy as jnp
        import numpy as np
        B, F0, D = (256, 39, 16)
        LAYER_SIZES = [128, 128, 128]
        key = jax.random.key(seed)
        ks = jax.random.split(key, 1 + 2 * len(LAYER_SIZES))
        inputs = jax.random.normal(ks[0], (B, F0, D), dtype=jnp.float32)
        out = {'inputs': inputs}
        field_nums = [F0]
        for i, size in enumerate(LAYER_SIZES):
            fk = field_nums[-1]
            fan_in = F0 * fk
            scale = np.sqrt(2.0 / (fan_in + size)).astype(np.float32)
            out[f'w{i}'] = jax.random.normal(ks[1 + 2 * i], (F0, fk, size), dtype=jnp.float32) * scale
            out[f'b{i}'] = jnp.zeros((size,), dtype=jnp.float32)
            field_nums.append(size // 2)
        return out
    _L0_rec_all = _L0_rec_setup()
    _L0_rec_in = {k: v for k, v in _L0_rec_all.items() if k in ('w0', 'w1', 'w2', 'b0', 'b1', 'b2')}
    del _L0_rec_all
    return {'dense_ctx': dense_ctx, 'ids': ids, 'tbl_0': tbl_0, 'tbl_1': tbl_1, 'tbl_2': tbl_2, 'tbl_3': tbl_3, 'tbl_4': tbl_4, 'tbl_5': tbl_5, 'tbl_6': tbl_6, 'tbl_7': tbl_7, 'tbl_8': tbl_8, 'tbl_9': tbl_9, 'tbl_10': tbl_10, 'tbl_11': tbl_11, 'tbl_12': tbl_12, 'tbl_13': tbl_13, 'tbl_14': tbl_14, 'tbl_15': tbl_15, 'tbl_16': tbl_16, 'tbl_17': tbl_17, 'tbl_18': tbl_18, 'tbl_19': tbl_19, 'tbl_20': tbl_20, 'tbl_21': tbl_21, 'tbl_22': tbl_22, 'tbl_23': tbl_23, 'tbl_24': tbl_24, 'tbl_25': tbl_25, 'tbl_26': tbl_26, 'tbl_27': tbl_27, 'tbl_28': tbl_28, 'tbl_29': tbl_29, 'tbl_30': tbl_30, 'tbl_31': tbl_31, 'tbl_32': tbl_32, 'tbl_33': tbl_33, 'tbl_34': tbl_34, 'tbl_35': tbl_35, 'tbl_36': tbl_36, 'tbl_37': tbl_37, 'tbl_38': tbl_38, 'W_top1': W_top1, 'b_top1': b_top1, 'W_top2': W_top2, 'b_top2': b_top2, 'W_top3': W_top3, 'L0_rec_w0': _L0_rec_in['w0'], 'L0_rec_w1': _L0_rec_in['w1'], 'L0_rec_w2': _L0_rec_in['w2'], 'L0_rec_b0': _L0_rec_in['b0'], 'L0_rec_b1': _L0_rec_in['b1'], 'L0_rec_b2': _L0_rec_in['b2']}

def reference(dense_ctx, ids, tbl_0, tbl_1, tbl_2, tbl_3, tbl_4, tbl_5, tbl_6, tbl_7, tbl_8, tbl_9, tbl_10, tbl_11, tbl_12, tbl_13, tbl_14, tbl_15, tbl_16, tbl_17, tbl_18, tbl_19, tbl_20, tbl_21, tbl_22, tbl_23, tbl_24, tbl_25, tbl_26, tbl_27, tbl_28, tbl_29, tbl_30, tbl_31, tbl_32, tbl_33, tbl_34, tbl_35, tbl_36, tbl_37, tbl_38, W_top1, b_top1, W_top2, b_top2, W_top3, L0_rec_w0, L0_rec_w1, L0_rec_w2, L0_rec_b0, L0_rec_b1, L0_rec_b2):
    import jax
    import jax.numpy as jnp

    def _L0_rec_ref(inputs, w0, w1, w2, b0, b1, b2):
        import jax, jax.numpy as jnp
        import numpy as np
        B, F0, D = (256, 39, 16)
        LAYER_SIZES = [128, 128, 128]
        x0 = inputs
        xk = inputs
        params = [(w0, b0), (w1, b1), (w2, b2)]
        n_layers = len(params)
        direct = []
        for idx, (W, b) in enumerate(params):
            z = jnp.einsum('bhd,bkd,hks->bsd', x0, xk, W) + b[None, :, None]
            z = jax.nn.relu(z)
            if idx != n_layers - 1:
                half = z.shape[1] // 2
                xk = z[:, :half, :]
                direct.append(z[:, half:, :])
            else:
                direct.append(z)
        logit = jnp.sum(jnp.concatenate(direct, axis=1), axis=-1)
        return logit
    e = jnp.stack([tbl_0[ids[:, 0]], tbl_1[ids[:, 1]], tbl_2[ids[:, 2]], tbl_3[ids[:, 3]], tbl_4[ids[:, 4]], tbl_5[ids[:, 5]], tbl_6[ids[:, 6]], tbl_7[ids[:, 7]], tbl_8[ids[:, 8]], tbl_9[ids[:, 9]], tbl_10[ids[:, 10]], tbl_11[ids[:, 11]], tbl_12[ids[:, 12]], tbl_13[ids[:, 13]], tbl_14[ids[:, 14]], tbl_15[ids[:, 15]], tbl_16[ids[:, 16]], tbl_17[ids[:, 17]], tbl_18[ids[:, 18]], tbl_19[ids[:, 19]], tbl_20[ids[:, 20]], tbl_21[ids[:, 21]], tbl_22[ids[:, 22]], tbl_23[ids[:, 23]], tbl_24[ids[:, 24]], tbl_25[ids[:, 25]], tbl_26[ids[:, 26]], tbl_27[ids[:, 27]], tbl_28[ids[:, 28]], tbl_29[ids[:, 29]], tbl_30[ids[:, 30]], tbl_31[ids[:, 31]], tbl_32[ids[:, 32]], tbl_33[ids[:, 33]], tbl_34[ids[:, 34]], tbl_35[ids[:, 35]], tbl_36[ids[:, 36]], tbl_37[ids[:, 37]], tbl_38[ids[:, 38]]], axis=1)
    z = _L0_rec_ref(e, L0_rec_w0, L0_rec_w1, L0_rec_w2, L0_rec_b0, L0_rec_b1, L0_rec_b2)
    z = z.reshape(z.shape[0], -1)
    h = jnp.concatenate([z, dense_ctx], axis=1)
    h = jnp.maximum(h @ W_top1 + b_top1, 0.0)
    h = jnp.maximum(h @ W_top2 + b_top2, 0.0)
    y = h @ W_top3
    return y

_drawn_inputs = setup_inputs


def setup_inputs(seed=0):
    import zlib

    import numpy as np

    out = dict(_drawn_inputs(seed))
    spreads = {'b_top1': (0.0, 2.0),
     'b_top2': (0.0, 2.0),
     'L0_rec_b0': (0.0, 0.346),
     'L0_rec_b1': (0.0, 0.527),
     'L0_rec_b2': (0.0, 0.8)}
    factors = {'tbl_0': 8.0,
     'tbl_1': 8.0,
     'tbl_2': 8.0,
     'tbl_3': 8.0,
     'tbl_4': 8.0,
     'tbl_5': 8.0,
     'tbl_6': 8.0,
     'tbl_7': 8.0,
     'tbl_8': 8.0,
     'tbl_9': 8.0,
     'tbl_10': 8.0,
     'tbl_11': 8.0,
     'tbl_12': 8.0,
     'tbl_13': 8.0,
     'tbl_14': 8.0,
     'tbl_15': 8.0,
     'tbl_16': 8.0,
     'tbl_17': 8.0,
     'tbl_18': 8.0,
     'tbl_19': 8.0,
     'tbl_20': 8.0,
     'tbl_21': 8.0,
     'tbl_22': 8.0,
     'tbl_23': 8.0,
     'tbl_24': 8.0,
     'tbl_25': 8.0,
     'tbl_26': 8.0,
     'tbl_27': 8.0,
     'tbl_28': 8.0,
     'tbl_29': 8.0,
     'tbl_30': 8.0,
     'tbl_31': 8.0,
     'tbl_32': 8.0,
     'tbl_33': 8.0,
     'tbl_34': 8.0,
     'tbl_35': 8.0,
     'tbl_36': 8.0,
     'tbl_37': 8.0,
     'tbl_38': 8.0,
     'L0_rec_w0': 8.0,
     'L0_rec_w1': 6.219,
     'L0_rec_w2': 4.701,
     'dense_ctx': 8.0}
    for name, (base, spread) in spreads.items():
        noise = np.random.default_rng([zlib.crc32(name.encode()), seed]).standard_normal(out[name].shape)
        drawn = base * np.exp(spread * noise) if base else spread * noise
        out[name] = jnp.asarray(drawn.astype(out[name].dtype))
    for name, factor in factors.items():
        out[name] = (out[name] * factor).astype(out[name].dtype)
    return out
```

```python
import concourse.bass as bass
from concourse import mybir
from contextlib import ExitStack

F32 = mybir.dt.float32
F32R = mybir.dt.float32r
I32 = mybir.dt.int32
ALU = mybir.AluOpType
ACT = mybir.ActivationFunctionType

BATCH, NF, D, S, K1 = 2048, 39, 16, 128, 64
DENSE, H1, H2 = 16, 512, 256
TB = 128
TILES = BATCH // TB
DC = 4
CPT = D // DC
N = DC * TB
R2 = 2 * NF
NO = 3
R0 = NO * NF
T0 = 7
LAST0 = 2 * NF
T1 = 20

P1, P0, P2 = 10, 4, 10
STEPS = P1 + P0 + P2
L1, L0, L2 = 0, P1, P1 + P0
SPLIT = set()
SEL_AHEAD, COPY_AHEAD = 6, 4
SEL_AHEAD0 = 2
RING = 4
AUX_T, AUX_B = 2, 6
COPY_T, COPY_B = 6, 9
RELU0_AT = 17
SPL = sorted(SPLIT)
NS = len(SPL)
PLAIN = [k for k in range(STEPS) if k not in SPLIT and not L0 <= k < L2]
SELS = P1 + P0
CREDIT = 2
Z_CREDIT = 1
FOLD_CREDIT = 9


def step_no(c, k, last=False):
    return P0 + STEPS * c + k - (P0 if last and k >= L2 else 0)


def splits_to(c, k):
    return NS * c + sum(1 for s in SPL if s <= k)


def group_no(c, layer, last=False):
    return 3 * c + {1: 1, 0: 2, 2: 2 if last else 3}[layer]


PT = dict(step=STEPS * CPT, split=NS * CPT, group=3 * CPT, sel=SELS * CPT, copy=P1 * CPT, aux=2 * CPT)


def build(nc, ids, tables, sel_d, w0a_d, w0b_d, w1_d, w2_d, b_d, dense_d, wt1_d, bt1_d, wt2_d, bt2_d, wt3_d, out):
    ctx = ExitStack()
    with ctx:
        def sb(name, shape, dt=F32):
            return ctx.enter_context(nc.sbuf_tensor(name, shape, dt))

        def pb(name, shape):
            return ctx.enter_context(nc.psum_tensor(name, shape, F32))

        def sem(name):
            return ctx.enter_context(nc.semaphore(name))

        ids_sb = sb("ids_sb", [TB, TILES, NF], I32)
        idx = sb("idx", [TB, NF], I32)
        emb = sb("emb", [TB, NF, D])
        emb2 = sb("emb2", [TB, D, 2, NF])
        x2 = sb("x2", [R2, 2, N], F32R)
        sel = sb("sel", [R2, T0 + 1 + T1, 128], F32R)
        base = sb("base", [R0, N])
        xb = sb("xb", [128, T1, N])
        xk1 = sb("xk1", [128, N])
        xk2 = sb("xk2", [128, N])
        P = sb("P", [128, RING, 2, N])
        Ph = sb("Ph", [128, RING if NS else 1, 2, N if NS else 2], F32R)
        Pl = sb("Pl", [128, RING if NS else 1, 2, N if NS else 2], F32R)
        w0 = sb("w0", [R0, T0, S])
        wp = sb("wp", [128, len(PLAIN), 2, S])
        wh = sb("wh", [128, max(NS, 1), 2, S], F32R)
        wl = sb("wl", [128, max(NS, 1), 2, S], F32R)
        bias = sb("bias", [S, 3])
        direct = sb("direct", [128, 3, DC, TB])
        half = sb("half", [128, 2, TB])
        feat = sb("feat", [128, 2, BATCH])
        ident = sb("ident", [128, 128])
        wt1 = sb("wt1", [128, 2, H1])
        wt1d = sb("wt1d", [DENSE, H1])
        wt2 = sb("wt2", [128, H1 // 128, H2])
        wt3 = sb("wt3", [128, H2 // 128])
        bt1 = sb("bt1", [128, H1 // 128])
        bt2 = sb("bt2", [128, H2 // 128])
        y_sb = sb("y_sb", [1, BATCH])
        xflat = xb[:, :, :].rearrange("p t n -> p (t n)")
        n_sel = (T0 + 1 + T1) * 128
        sel_st = xflat[0:R2, 0:n_sel].rearrange("p (t m) -> p t m", m=128)
        w0b_st = xflat[0:R0, n_sel:n_sel + T0 * S].rearrange("p (t m) -> p t m", m=S)
        o = n_sel + T0 * S
        w_st = xflat[:, o:o + max(NS, 1) * 2 * S].rearrange("p (q j m) -> p q j m", j=2, m=S)
        h1 = xb[:, 0:8, :].rearrange("p (u m) n -> p u m n", u=2)
        h2 = xb[:, 8:12, :].rearrange("p (u m) n -> p u m n", u=2)
        dense = xb[0:DENSE, 12:16, :].rearrange("p t n -> p (t n)")

        xb_ps = pb("xb_ps", [128, 2, 2, N])
        z_ps = pb("z_ps", [128, 2, N])
        aux_ps = pb("aux_ps", [128, N])

        ids_in = sem("ids_in")
        weights_in = sem("weights_in")
        weights_act = sem("weights_act")
        weights_ready = sem("weights_ready")
        idx_ready = sem("idx_ready")
        gathered = sem("gathered")
        high_done = sem("high_done")
        emb2_ready = sem("emb2_ready")
        aux_ready = sem("aux_ready")
        aux_copied = sem("aux_copied")
        sel_ready = sem("sel_ready")
        xb_copied = sem("xb_copied")
        products = sem("products")
        rounded = sem("rounded")
        low_ready = sem("low_ready")
        steps_done = sem("steps_done")
        xk1_ready = sem("xk1_ready")
        xk2_ready = sem("xk2_ready")
        z_read = sem("z_read")
        folds = sem("folds")
        dense_in = sem("dense_in")
        m1_ready = sem("m1_ready")
        m1_read = sem("m1_read")
        m2_ready = sem("m2_ready")
        m2_read = sem("m2_read")
        m3_ready = sem("m3_ready")
        m3_read = sem("m3_read")
        out_done = sem("out_done")
        settled = sem("settled")

        block = ctx.enter_context(nc.Block())
        w12 = {1: w1_d, 2: w2_d}

        def dram_pair(k):
            layer, p = (1, k) if k < L0 else (2, k - L2)
            return w12[layer][:, 2 * p:2 * p + 2, :]

        n_loads = 4 + len(PLAIN) + NS + 6

        @block.sync
        def _(sp):
            sp.dma_start(ids_sb[:, :, :], ids.rearrange("(t p) f -> p t f", p=TB)).then_inc(ids_in, 16)
            sp.dma_start(sel_st, sel_d).then_inc(weights_in, 16)
            sp.dma_start(w0[:, :, :], w0a_d).then_inc(weights_in, 16)
            sp.dma_start(w0b_st, w0b_d).then_inc(weights_in, 16)
            sp.dma_start(bias[:, :], b_d).then_inc(weights_in, 16)
            for q, k in enumerate(SPL):
                sp.dma_start(w_st[:, q], dram_pair(k)).then_inc(weights_in, 16)
            for q, k in enumerate(PLAIN):
                sp.dma_start(wp[:, q], dram_pair(k)).then_inc(weights_in, 16)
            sp.dma_start(wt1[:, :, :], wt1_d[0:256, :].rearrange("(t p) n -> p t n", p=128)).then_inc(weights_in, 16)
            sp.dma_start(wt1d[:, :], wt1_d[256:272, :]).then_inc(weights_in, 16)
            sp.dma_start(wt2[:, :, :], wt2_d.rearrange("(t p) n -> p t n", p=128)).then_inc(weights_in, 16)
            sp.dma_start(wt3[:, :], wt3_d).then_inc(weights_in, 16)
            sp.dma_start(bt1[:, :], bt1_d).then_inc(weights_in, 16)
            sp.dma_start(bt2[:, :], bt2_d).then_inc(weights_in, 16)
            sp.wait_ge(products, CREDIT + TILES * PT["step"])
            sp.dma_start(dense, dense_d).then_inc(dense_in, 16)
            sp.wait_ge(m3_read, BATCH // N)
            sp.dma_start(out.rearrange("(a n) o -> a (n o)", a=1), y_sb[:, :]).then_inc(out_done, 16)
            sp.wait_ge(out_done, 16)

        @block.gpsimd
        def _(pool):
            for layer in range(3):
                pool.memset(direct[:, layer], 0.0).then_inc(folds, 3)
            pool.memset(ident[:, :], 0.0).then_inc(idx_ready, 1)
            pool.wait_ge(idx_ready, 1)
            pool.affine_select(out=ident[:, :], in_=ident[:, :], compare_op=ALU.not_equal, fill=1.0, base=0,
                               pattern=[[-1, 128]], channel_multiplier=1).then_inc(idx_ready, 1)
            pool.wait_ge(ids_in, 16)

            def settle():
                pool.sem_inc(settled, 1)

            def pick_ids(T):
                settle()
                pool.tensor_copy(idx[:, :], ids_sb[:, bass.ds(T, 1), :].rearrange("p a f -> p (a f)"))\
                    .then_inc(idx_ready, 1)
                pool.wait_ge(idx_ready, T + 3)
                settle()

            def gather(f):
                pool.indirect_dma_start(emb[:, f, :], None, tables[f],
                                        bass.IndirectOffsetOnAxis(ap=idx[:, f:f + 1], axis=0)).then_inc(gathered, 16)

            def split_emb(T):
                pool.wait_ge(gathered, (T + 1) * (16 * NF))
                settle()
                src = emb[:, :, :].rearrange("p f d -> p d f")
                pool.tensor_copy(emb2[:, :, 0, :].bitcast(F32R), src).then_inc(high_done, 1)
                pool.wait_ge(high_done, T + 1)
                pool.tensor_tensor(emb2[:, :, 1, :].bitcast(F32R), src, emb2[:, :, 0, :], ALU.subtract)\
                    .then_inc(emb2_ready, 1)

            def fold(n, layer, T, q):
                rows, col = {0: (slice(0, K1), 0), 1: (slice(K1, S), 0), 2: (slice(0, S), 1)}[layer]
                pool.wait_ge(z_read, Z_CREDIT + n + 1)
                r = direct[rows, layer]
                h = half[rows]
                f = feat[rows, col, bass.ds(T * TB, TB)]
                pool.tensor_tensor(h, r[:, 0:2], r[:, 2:4], ALU.add).then_inc(folds, 1)
                pool.wait_ge(folds, FOLD_CREDIT + 3 * n + 1)
                settle()
                if q == 0:
                    pool.tensor_tensor(f, h[:, 0], h[:, 1], ALU.add).then_inc(folds, 2)
                else:
                    pool.tensor_tensor(f, f, h[:, 0], ALU.add).then_inc(folds, 1)
                    pool.wait_ge(folds, FOLD_CREDIT + 3 * n + 2)
                    settle()
                    pool.tensor_tensor(f, f, h[:, 1], ALU.add).then_inc(folds, 1)
                pool.wait_ge(folds, FOLD_CREDIT + 3 * n + 3)
                settle()

            pick_ids(0)
            for f in range(NF):
                gather(f)
            split_emb(0)
            fold(0, 0, 0, 0)

            def tile(T, last):
                if not last:
                    pool.wait_ge(emb2_ready, T + 1)
                    pick_ids(T + 1)
                for c in range(CPT):
                    end = last and c == CPT - 1
                    G = T * PT["group"]
                    fold(G + group_no(c, 1), 1, T, c)
                    if not end:
                        fold(G + group_no(c, 0), 0, T + (c + 1) // CPT, (c + 1) % CPT)
                    if not last and c < 3:
                        for f in range(13 * c, 13 * c + 13):
                            gather(f)
                        pool.wait_ge(gathered, 16 * (NF * (T + 1) + 13 * (c + 1)))
                    if not last and c == 2:
                        pool.wait_ge(aux_ready, T * PT["aux"] + 2 * c + 3)
                        split_emb(T + 1)
                    fold(G + group_no(c, 2, end), 2, T, c)

            with pool.Fori(0, TILES - 1) as T:
                tile(T, False)
            tile(TILES - 1, True)

        @block.scalar
        def _(act):
            act.wait_ge(weights_in, 16 * n_loads)
            act.activation(sel[:, :, :], sel_st, ACT.Copy).then_inc(weights_act, 1)
            act.activation(y_sb[0:1, 0:1], bias[0:1, 0:1], ACT.Copy).then_inc(z_read, Z_CREDIT)
            if NS:
                act.activation(wh[:, :, :, :], w_st, ACT.Copy).then_inc(weights_act, 1)

            def copy_aux(number, dst, rows):
                act.wait_ge(aux_ready, number + 1)
                act.activation(dst, aux_ps[0:rows, :], ACT.Copy).then_inc(aux_copied, 1)

            def copy_xb(T, c, p):
                act.wait_ge(sel_ready, T * PT["sel"] + P0 + SELS * c + p + 1)
                act.activation(xb[:, 2 * p:2 * p + 2, :], xb_ps[:, (P0 + SELS * c + p) % 2], ACT.Copy)\
                    .then_inc(xb_copied, 1)

            def relu(T, c, layer, last=False):
                n = group_no(c, layer, last) if c >= 0 else 0
                end = {1: L0, 0: L2, 2: STEPS}[layer] - 1
                z = z_ps[:, n % 2]
                act.wait_ge(steps_done, T * PT["step"] + step_no(c, end, last) + 1 if c >= 0 else P0)
                lo, hi = slice(0, K1), slice(K1, S)
                b = bias[:, layer:layer + 1]
                if layer < 2:
                    xk, ready = ((xk1, xk1_ready), (xk2, xk2_ready))[layer]
                    act.activation(xk[lo, :], z[lo], ACT.Relu, bias=b[lo])
                    act.activation(xk[hi, :], z[lo], ACT.Relu, bias=b[lo]).then_inc(ready, 1)
                rows_in = slice(0, S) if layer == 2 else hi
                rows_out = (lo, hi, slice(0, S))[layer]
                n = T * PT["group"] + n
                if c >= 0:
                    act.wait_ge(folds, FOLD_CREDIT + 3 * (n - (2 if layer == 0 or (last and layer == 2) else 3)) + 1)
                else:
                    act.wait_ge(folds, FOLD_CREDIT)
                act.activation(direct[rows_out, layer].rearrange("p d b -> p (d b)"), z[rows_in], ACT.Relu,
                               bias=b[rows_in]).then_inc(z_read, 1)

            copy_aux(0, x2[:, 0, :], R2)
            copy_aux(1, base[:, :], R0)
            act.wait_ge(weights_ready, 1 + bool(NS))
            for p in range(COPY_AHEAD):
                copy_xb(0, 0, p)
            relu(0, -1, 0)

            def tile(T, last):
                for c in range(CPT):
                    end = last and c == CPT - 1
                    for k in range(STEPS):
                        if end and L0 <= k < L2:
                            continue
                        if k + COPY_AHEAD < P1:
                            p = k + COPY_AHEAD
                            act.wait_ge(products, T * PT["step"] + step_no(c - 1, L2 + p) + 1 + CREDIT)
                            copy_xb(T, c, p)
                        if k + COPY_AHEAD >= STEPS and not end:
                            p = k + COPY_AHEAD - STEPS
                            act.wait_ge(products, T * PT["step"] + step_no(c, L2 + p) + 1 + CREDIT)
                            copy_xb(T, c + 1, p)
                        if k == COPY_T and not end:
                            copy_aux(T * PT["aux"] + 2 * c + 2, x2[:, (c + 1) % 2, :], R2)
                        if k == COPY_B and not end:
                            copy_aux(T * PT["aux"] + 2 * c + 3, base[:, :], R0)
                        if k in SPLIT:
                            s = step_no(c, k, end)
                            act.wait_ge(products, T * PT["step"] + s + 1 + CREDIT)
                            act.activation(Ph[:, s % RING], P[:, s % RING], ACT.Copy).then_inc(rounded, 1)
                        if k == L0 - 1:
                            relu(T, c, 1, end)
                        if k == RELU0_AT and not end:
                            relu(T, c, 0)
                        if k == STEPS - 1:
                            relu(T, c, 2, end)

            with act.Fori(0, TILES - 1) as T:
                tile(T, False)
            tile(TILES - 1, True)

            for s in range(BATCH // N + 2):
                if s < BATCH // N:
                    for m in range(H1 // 128):
                        act.wait_ge(m1_ready, 4 * s + m + 1)
                        if s >= 2:
                            act.wait_ge(m2_ready, 2 * (s - 1))
                        act.activation(h1[:, s % 2, m, :], xb_ps[:, m // 2, m % 2, :], ACT.Relu,
                                       bias=bt1[:, m:m + 1]).then_inc(m1_read, 1)
                if 1 <= s <= BATCH // N:
                    for m in range(H2 // 128):
                        act.wait_ge(m2_ready, 2 * (s - 1) + m + 1)
                        if s >= 3:
                            act.wait_ge(m3_ready, s - 2)
                        act.activation(h2[:, (s - 1) % 2, m, :], z_ps[:, m, :], ACT.Relu,
                                       bias=bt2[:, m:m + 1]).then_inc(m2_read, 1)
                if s >= 2:
                    act.wait_ge(m3_ready, s - 1)
                    act.activation(y_sb[0:1, (s - 2) * N:(s - 1) * N], aux_ps[0:1, :], ACT.Copy).then_inc(m3_read, 1)

        @block.vector
        def _(dve):
            dve.memset(half[:, 0, 0:1], 0.0).then_inc(products, CREDIT)
            dve.wait_ge(weights_in, 16 * n_loads)
            dve.tensor_tensor(w0[:, :, :], w0[:, :, :], w0b_st, ALU.add).then_inc(weights_ready, 1)
            if NS:
                dve.wait_ge(weights_act, 2)
                dve.tensor_tensor(wl[:, :, :, :], w_st, wh[:, :, :, :], ALU.subtract).then_inc(weights_ready, 1)

            def product(s, T, k, c):
                out_ = P[:, s % RING]
                if k < L0:
                    dve.wait_ge(xb_copied, T * PT["copy"] + P1 * c + k + 1)
                    a, b, rows = xb[:, 2 * k:2 * k + 2, :], xk1, 128
                elif k < L2:
                    j = k - L0
                    if c < 0:
                        dve.wait_ge(sel_ready, j + 1)
                        a = xb_ps[:, j % 2]
                    else:
                        dve.wait_ge(sel_ready, T * PT["sel"] + P0 + SELS * c + P1 + j + 1)
                        a = xb_ps[:, (P0 + SELS * c + P1 + j) % 2]
                    b, rows = base, R0
                else:
                    a, b, rows = xb[:, 2 * (k - L2):2 * (k - L2) + 2, :], xk2, 128
                n = 2
                if k == L2 - 1:
                    rows, n = LAST0, 1
                dve.tensor_tensor(out_[0:rows, 0:n], a[0:rows, 0:n],
                                  b[0:rows, :].unsqueeze(1).broadcast_to([rows, n, N]), ALU.mult)\
                    .then_inc(products, 1)

            dve.wait_ge(aux_copied, 2)
            for j in range(P0):
                product(j, 0, L0 + j, -1)

            def tile(T, last):
                for c in range(CPT):
                    end = last and c == CPT - 1
                    for k in range(STEPS):
                        if end and L0 <= k < L2:
                            continue
                        s = step_no(c, k, end)
                        if k == L1:
                            dve.wait_ge(xk1_ready, T * CPT + c + 1)
                        if k == L0:
                            dve.wait_ge(aux_copied, T * PT["aux"] + 2 * c + 4)
                        if k == L2:
                            dve.wait_ge(xk2_ready, T * CPT + c + 1)
                        dve.wait_ge(steps_done, T * PT["step"] + s - RING + 1)
                        product(s, T, k, c)
                        if k - 1 in SPLIT:
                            r = s - 1
                            dve.wait_ge(rounded, T * PT["split"] + splits_to(c, k - 1))
                            dve.tensor_tensor(Pl[:, r % RING], P[:, r % RING], Ph[:, r % RING], ALU.subtract)\
                                .then_inc(low_ready, 1)

            with dve.Fori(0, TILES - 1) as T:
                tile(T, False)
            tile(TILES - 1, True)

        @block.tensor
        def _(pe):
            def select(number, which, tiles, rows, wait):
                if wait:
                    pe.wait_ge(*wait)
                for j, t in enumerate(tiles):
                    m = pe.matmul(xb_ps[0:rows, number % 2, j, :], sel[:, t, 0:rows], which, start=True, stop=True)
                m.then_inc(sel_ready, 1)

            def tiles0(j):
                return [2 * j, 2 * j + 1] if j < P0 - 1 else [2 * j]

            def transposes(c, quarter):
                for d in range(DC):
                    m = pe.transpose(aux_ps[0:R2, d * TB:(d + 1) * TB],
                                     emb2[:, quarter * DC + d, :, :].rearrange("p a f -> p (a f)"), ident[:, :])
                m.then_inc(aux_ready, 1)

            def base_rows(slot):
                pe.matmul(aux_ps[0:R0, :], sel[:, T0, 0:R0], x2[:, slot, :], start=True, stop=True)\
                    .then_inc(aux_ready, 1)

            def contract0(s, j, z):
                for i, t in enumerate(tiles0(j)):
                    rows = LAST0 if t == T0 - 1 else R0
                    m = pe.matmul(z, w0[0:rows, t, :], P[0:rows, s % RING, i, :], start=t == 0, stop=t == T0 - 1)
                m.then_inc(steps_done, 1)

            pe.wait_ge(idx_ready, 2)
            pe.wait_ge(emb2_ready, 1)
            transposes(-1, 0)
            pe.wait_ge(weights_act, 1 + bool(NS))
            pe.wait_ge(weights_ready, 1 + bool(NS))
            pe.wait_ge(weights_in, 16 * n_loads)
            pe.wait_ge(aux_copied, 1)
            base_rows(0)
            for j in range(P0):
                if j < 2:
                    select(j, x2[:, 0, :], tiles0(j), R0, None)
            for j in range(P0):
                pe.wait_ge(products, CREDIT + j + 1)
                contract0(j, j, z_ps[:, 0, :])
                if j + 2 < P0:
                    select(j + 2, x2[:, 0, :], tiles0(j + 2), R0, None)
            for p in range(SEL_AHEAD):
                wait = (products, CREDIT + p + 3) if p < 2 else (xb_copied, p - 1)
                select(P0 + p, x2[:, 0, :], [T0 + 1 + 2 * p, T0 + 2 + 2 * p], 128, wait)

            def tile(T, last):
                for c in range(CPT):
                    end = last and c == CPT - 1

                    def select1(cc, p):
                        if p < 2:
                            wait = (products, T * PT["step"] + step_no(cc - 1, L0 + P0 - 2 + p) + 1 + CREDIT)
                        else:
                            wait = (xb_copied, T * PT["copy"] + P1 * cc + p - 1)
                        select(P0 + SELS * cc + p, x2[:, cc % 2, :], [T0 + 1 + 2 * p, T0 + 2 + 2 * p], 128, wait)

                    for k in range(STEPS):
                        if end and L0 <= k < L2:
                            continue
                        if k + SEL_AHEAD < P1:
                            select1(c, k + SEL_AHEAD)
                        if k + SEL_AHEAD >= STEPS and not end:
                            select1(c + 1, k + SEL_AHEAD - STEPS)
                        if L0 <= k + SEL_AHEAD0 < L2 and not end:
                            j = k + SEL_AHEAD0 - L0
                            if j < 2:
                                wait = (xb_copied, T * PT["copy"] + P1 * c + P1 - 1 + j)
                            else:
                                wait = (products, T * PT["step"] + step_no(c, L0 + j - 2) + 1 + CREDIT)
                            select(P0 + SELS * c + P1 + j, x2[:, (c + 1) % 2, :], tiles0(j), R0, wait)
                        if k == AUX_T and not end:
                            pe.wait_ge(emb2_ready, T + 1 + (c + 1) // CPT)
                            pe.wait_ge(aux_copied, T * PT["aux"] + 2 * c + 2)
                            transposes(c, (c + 1) % CPT)
                        if k == AUX_B and not end:
                            pe.wait_ge(aux_copied, T * PT["aux"] + 2 * c + 3)
                            base_rows((c + 1) % 2)
                        layer = 1 if k < L0 else 0 if k < L2 else 2
                        n = group_no(c, layer, end)
                        z = z_ps[:, n % 2, :]
                        s = step_no(c, k, end)
                        first = k in (L1, L0, L2)
                        if first:
                            pe.wait_ge(z_read, Z_CREDIT + T * PT["group"] + n - 1)
                        if layer == 0:
                            pe.wait_ge(products, T * PT["step"] + s + 1 + CREDIT)
                            contract0(s, k - L0, z)
                            continue
                        final = k in (L0 - 1, STEPS - 1)
                        if k not in SPLIT:
                            pe.wait_ge(products, T * PT["step"] + s + 1 + CREDIT)
                            for j in range(2):
                                m = pe.matmul(z, wp[:, PLAIN.index(k), j, :], P[:, s % RING, j, :],
                                              start=first and j == 0, stop=final and j == 1)
                        else:
                            q = SPL.index(k)
                            pe.wait_ge(rounded, T * PT["split"] + splits_to(c, k))
                            for j in range(2):
                                for i, w in enumerate((wh, wl)):
                                    pe.matmul(z, w[:, q, j, :], Ph[:, s % RING, j, :],
                                              start=first and i + j == 0, stop=False)
                            pe.wait_ge(low_ready, T * PT["split"] + splits_to(c, k))
                            for j in range(2):
                                m = pe.matmul(z, wh[:, q, j, :], Pl[:, s % RING, j, :], start=False,
                                              stop=final and j == 1)
                        m.then_inc(steps_done, 1)

            with pe.Fori(0, TILES - 1) as T:
                tile(T, False)
            tile(TILES - 1, True)

            groups = TILES * PT["group"]
            pe.wait_ge(z_read, Z_CREDIT + groups)
            pe.wait_ge(folds, FOLD_CREDIT + 3 * groups)
            for s in range(BATCH // N + 2):
                if s < BATCH // N:
                    cols = slice(s * N, (s + 1) * N)
                    for m in range(H1 // 128):
                        if s:
                            pe.wait_ge(m1_read, 4 * (s - 1) + m + 1)
                        o_ = xb_ps[:, m // 2, m % 2, :]
                        for t in range(2):
                            pe.matmul(o_, wt1[:, t, m * 128:(m + 1) * 128], feat[:, t, cols], start=t == 0, stop=False)
                        if s == 0 and m == 0:
                            pe.wait_ge(dense_in, 16)
                        pe.matmul(o_, wt1d[:, m * 128:(m + 1) * 128], dense[:, cols], start=False, stop=True)\
                            .then_inc(m1_ready, 1)
                if 1 <= s <= BATCH // N:
                    pe.wait_ge(m1_read, 4 * s)
                    for m in range(H2 // 128):
                        if s >= 2:
                            pe.wait_ge(m2_read, 2 * (s - 2) + m + 1)
                        for t in range(H1 // 128):
                            i = pe.matmul(z_ps[:, m, :], wt2[:, t, m * 128:(m + 1) * 128], h1[:, (s - 1) % 2, t, :],
                                          start=t == 0, stop=t == H1 // 128 - 1)
                        i.then_inc(m2_ready, 1)
                if s >= 2:
                    pe.wait_ge(m2_read, 2 * (s - 1))
                    if s >= 3:
                        pe.wait_ge(m3_read, s - 2)
                    for t in range(H2 // 128):
                        i = pe.matmul(aux_ps[0:1, :], wt3[:, t:t + 1], h2[:, (s - 2) % 2, t, :],
                                      start=t == 0, stop=t == H2 // 128 - 1)
                    i.then_inc(m3_ready, 1)


def kernel(**inputs):
    import numpy as np
    import concourse.bacc as bacc
    from concourse.bass_utils import run_bass_kernel_spmd

    a = {k: np.ascontiguousarray(v) for k, v in inputs.items()}
    sel = np.zeros((2, NF, T0 + 1 + T1, 128), np.float32)
    for t in range(T0 + 1):
        for r in range(NO):
            offset = NO * t + r if t < T0 else 0
            for i in range(NF):
                sel[:, (i + offset) % NF, t, r * NF + i] = 1
    for t in range(T1):
        for j in range(2):
            sel[:, min(2 * t + j, NF - 1), T0 + 1 + t, j * K1:(j + 1) * K1] = 1
    w = a["L0_rec_w0"]
    w0a = np.zeros((NO, NF, T0, S), w.dtype)
    w0b = np.zeros((NO, NF, T0, S), w.dtype)
    i = np.arange(NF)
    for t in range(T0):
        for r in range(NO):
            offset = NO * t + r
            if offset <= NF // 2:
                w0a[r, :, t] = w[i, (i + offset) % NF]
                if offset:
                    w0b[r, :, t] = w[(i + offset) % NF, i]

    def tiled(w):
        p = np.zeros((2 * T1, K1, S), w.dtype)
        p[:NF] = w
        return np.ascontiguousarray(p.reshape(T1, 2 * K1, S).transpose(1, 0, 2))

    arrays = {
        "ids": a["ids"],
        "sel": sel.reshape(R2, T0 + 1 + T1, 128),
        "w0a": w0a.reshape(R0, T0, S), "w0b": w0b.reshape(R0, T0, S),
        "w1": tiled(a["L0_rec_w1"]), "w2": tiled(a["L0_rec_w2"]),
        "b": np.ascontiguousarray(np.stack([a["L0_rec_b0"], a["L0_rec_b1"], a["L0_rec_b2"]], axis=1)),
        "dense": np.ascontiguousarray(a["dense_ctx"].T),
        "wt1": a["W_top1"], "bt1": np.ascontiguousarray(a["b_top1"].reshape(H1 // 128, 128).T),
        "wt2": a["W_top2"], "bt2": np.ascontiguousarray(a["b_top2"].reshape(H2 // 128, 128).T),
        "wt3": np.ascontiguousarray(a["W_top3"].reshape(H2 // 128, 128).T),
    }
    for f in range(NF):
        arrays[f"tbl_{f}"] = a[f"tbl_{f}"]
    nc = bacc.Bacc("TRN2", target_bir_lowering=False, num_devices=1)
    ap = {k: nc.dram_tensor(f"{k}_in", v.shape, mybir.dt.from_np(v.dtype), kind="ExternalInput").ap()
          for k, v in arrays.items()}
    out = nc.dram_tensor("y_out", (BATCH, 1), F32, kind="ExternalOutput").ap()
    build(nc, ap["ids"], [ap[f"tbl_{f}"] for f in range(NF)], ap["sel"], ap["w0a"], ap["w0b"], ap["w1"], ap["w2"],
          ap["b"], ap["dense"], ap["wt1"], ap["bt1"], ap["wt2"], ap["bt2"], ap["wt3"], out)
    return run_bass_kernel_spmd(nc, [{f"{k}_in": v for k, v in arrays.items()}], core_ids=[0]).results[0]["y_out"]
```

```python
import concourse.bass as bass
from concourse import mybir
from contextlib import ExitStack

F32 = mybir.dt.float32
F32R = mybir.dt.float32r
I32 = mybir.dt.int32
ALU = mybir.AluOpType
ACT = mybir.ActivationFunctionType

BATCH, NF, D, S, K1 = 2048, 39, 16, 128, 64
DENSE, H1, H2 = 16, 512, 256
TB = 128
TILES = BATCH // TB
DC = 4
CPT = D // DC
N = DC * TB
R2 = 2 * NF
NO = 3
R0 = NO * NF
T0 = 7
LAST0 = 2 * NF
T1 = 20
PAIRS = T1 // 2

PRE = 4
L1B, L2, STEPS = PAIRS - PRE, PAIRS, 2 * PAIRS
SPLIT = {0, 1, 2, 4, 5, 6, 7, 8, 10, 11, 12, 13, 15, 16, 17, 18}
SEL_AHEAD, COPY_AHEAD = 6, 4
assert SEL_AHEAD - 2 == PRE == COPY_AHEAD
RING = 4
XSLOTS = PAIRS + PRE
TRANSPOSE_AT, X2_AT = 0, 2
SUM_AT = [3, 5, 7, 9, 11, 12, 14]
SQUARE_LAG, CONTRACT_LAG = 2, 3
RELU2_AT, RELU1_AT, RELU0_AT = 3, 9, 19
SPL = sorted(SPLIT)
PLAIN = [k for k in range(STEPS) if k not in SPLIT]
NS, NS_PRE = len(SPL), sum(L1B <= k < L2 for k in SPL)
CREDIT = 2
FOLD_CREDIT = 9
Z_CREDIT = 1
AUX = 1 + T0

PER = dict(step=STEPS * CPT, split=NS * CPT, group=3 * CPT, sel=PAIRS * CPT, aux=AUX * CPT)


def step_no(c, k, end=False):
    return PRE + STEPS * c + k - (PRE if end and k >= L2 else 0)


def splits_to(c, k, end=False):
    return NS_PRE + NS * c + sum(s <= k for s in SPL) - (NS_PRE if end and k >= L2 else 0)


def group_no(c, layer, skipped=0):
    return 3 * c + {2: 0, 1: 1, 0: 2}[layer] - skipped


def x_slot(chunk, p):
    return PRE * (chunk % 2) + p if p < PRE else PRE + p


def build(nc, ids, tables, sel0_d, sel1_d, inc_d, w0a_d, w0b_d, w1_d, w2_d, b_d, dense_d, wt1_d, bt1_d, wt2_d, bt2_d,
          wt3_d, out):
    ctx = ExitStack()
    with ctx:
        def sb(name, shape, dt=F32):
            return ctx.enter_context(nc.sbuf_tensor(name, shape, dt))

        def pb(name, shape):
            return ctx.enter_context(nc.psum_tensor(name, shape, F32))

        def sem(name):
            return ctx.enter_context(nc.semaphore(name))

        ids_sb = sb("ids_sb", [TB, TILES, NF], I32)
        idx = sb("idx", [TB, NF], I32)
        emb = sb("emb", [TB, NF, D])
        emb2 = sb("emb2", [TB, D, 2, NF])
        x2 = sb("x2", [R2, 2, N], F32R)
        sel0 = sb("sel0", [R2, T0, R0], F32R)
        sel1 = sb("sel1", [R2, T1, 128], F32R)
        sq = sb("sq", [R0, 2, N])
        xb = sb("xb", [128, XSLOTS, 2, N])
        xk1 = sb("xk1", [128, 2, N])
        xk2 = sb("xk2", [128, N])
        P = sb("P", [128, RING, 2, N])
        Ph = sb("Ph", [128, RING, 2, N], F32R)
        Pl = sb("Pl", [128, RING, 2, N], F32R)
        w0 = sb("w0", [R0, T0, S])
        wp = sb("wp", [128, len(PLAIN), 2, S])
        wh = sb("wh", [128, NS, 2, S], F32R)
        wl = sb("wl", [128, NS, 2, S], F32R)
        bias = sb("bias", [S, 3])
        direct = sb("direct", [128, 3, DC, TB])
        half = sb("half", [128, 2, TB])
        feat = sb("feat", [128, 2, BATCH])
        ident = sb("ident", [128, 128])
        wt3 = sb("wt3", [128, H2 // 128])
        bt1 = sb("bt1", [128, H1 // 128])
        bt2 = sb("bt2", [128, H2 // 128])
        xflat = xb[:, :, :, :].rearrange("p q j n -> p (q j n)")
        at = [0]

        def stage(rows, a, b):
            at[0] += a * b
            return xflat[0:rows, at[0] - a * b:at[0]].rearrange("p (a b) -> p a b", b=b)

        sel0_st, sel1_st, inc = stage(R2, T0, R0), stage(R2, T1, 128), stage(R0, T0, NF)
        w0a_st, w0b_st = stage(R0, T0, S), stage(R0, T0, S)
        w_st = stage(128, NS, 2 * S).rearrange("p q (j m) -> p q j m", j=2)
        xt = xb[:, :, :, :].rearrange("p q j n -> p (q j) n")
        wt1 = xt[:, 0:2, :]
        wt1d = xt[0:DENSE, 2, :]
        wt2 = xt[:, 3:5, :].rearrange("p a (b n) -> p (a b) n", n=H2)
        h1 = xt[:, 8:16, :].rearrange("p (u m) n -> p u m n", u=2)
        dense = xt[0:DENSE, 16:20, :].rearrange("p t n -> p (t n)")
        h2 = xt[:, 20:24, :].rearrange("p (u m) n -> p u m n", u=2)
        y_sb = xt[0:1, 24:28, :].rearrange("p t n -> p (t n)")

        xb_ps = pb("xb_ps", [128, 2, 2, N])
        z_ps = pb("z_ps", [128, 2, N])
        z0_ps = pb("z0_ps", [128, N])
        aux_ps = pb("aux_ps", [128, N])

        ids_in = sem("ids_in")
        weights_in = sem("weights_in")
        parts_made = sem("parts_made")
        weights_made = sem("weights_made")
        incident = sem("incident")
        idx_ready = sem("idx_ready")
        gathered = sem("gathered")
        high_done = sem("high_done")
        emb2_ready = sem("emb2_ready")
        settled = sem("settled")
        aux_ready = sem("aux_ready")
        aux_read = sem("aux_read")
        sel_ready = sem("sel_ready")
        xb_copied = sem("xb_copied")
        products = sem("products")
        rounded = sem("rounded")
        low_ready = sem("low_ready")
        steps_done = sem("steps_done")
        squares_done = sem("squares_done")
        xk1_ready = sem("xk1_ready")
        xk2_ready = sem("xk2_ready")
        z_read = sem("z_read")
        folds = sem("folds")
        dense_in = sem("dense_in")
        mlp_in = sem("mlp_in")
        m1_ready = sem("m1_ready")
        m1_read = sem("m1_read")
        m2_ready = sem("m2_ready")
        m2_read = sem("m2_read")
        m3_ready = sem("m3_ready")
        m3_read = sem("m3_read")
        out_done = sem("out_done")

        block = ctx.enter_context(nc.Block())

        def dram_pair(k):
            if k >= L2:
                return w2_d[:, 2 * (k - L2):2 * (k - L2) + 2, :]
            p = (k + PRE) % PAIRS
            return w1_d[:, 2 * p:2 * p + 2, :]

        n_loads = 9 + STEPS
        all_steps = TILES * PER["step"]

        @block.sync
        def _(sp):
            sp.dma_start(ids_sb[:, :, :], ids.rearrange("(t p) f -> p t f", p=TB)).then_inc(ids_in, 16)
            for dst, src in ((w0a_st, w0a_d), (w0b_st, w0b_d), (inc, inc_d), (sel0_st, sel0_d), (sel1_st, sel1_d),
                             (bias[:, :], b_d), (wt3[:, :], wt3_d), (bt1[:, :], bt1_d), (bt2[:, :], bt2_d)):
                sp.dma_start(dst, src).then_inc(weights_in, 16)
            for q, k in enumerate(SPL):
                sp.dma_start(w_st[:, q], dram_pair(k)).then_inc(weights_in, 16)
            for q, k in enumerate(PLAIN):
                sp.dma_start(wp[:, q], dram_pair(k)).then_inc(weights_in, 16)
            sp.wait_ge(products, CREDIT + PRE + all_steps - STEPS)
            sp.dma_start(wt1, wt1_d[0:256, :].rearrange("(t p) n -> p t n", p=128)).then_inc(mlp_in, 16)
            sp.dma_start(wt1d, wt1_d[256:272, :]).then_inc(mlp_in, 16)
            sp.dma_start(wt2, wt2_d.rearrange("(t p) n -> p t n", p=128)).then_inc(mlp_in, 16)
            sp.wait_ge(products, CREDIT + all_steps - (PAIRS - PRE - 2))
            sp.dma_start(dense, dense_d).then_inc(dense_in, 16)
            sp.wait_ge(m3_read, BATCH // N)
            sp.dma_start(out.rearrange("(a n) o -> a (n o)", a=1), y_sb).then_inc(out_done, 16)
            sp.wait_ge(out_done, 16)

        @block.gpsimd
        def _(pool):
            for layer in range(3):
                pool.memset(direct[:, layer], 0.0).then_inc(folds, 3)
            pool.memset(ident[:, :], 0.0).then_inc(idx_ready, 1)
            pool.wait_ge(idx_ready, 1)
            pool.affine_select(out=ident[:, :], in_=ident[:, :], compare_op=ALU.not_equal, fill=1.0, base=0,
                               pattern=[[-1, 128]], channel_multiplier=1).then_inc(idx_ready, 1)
            pool.wait_ge(ids_in, 16)

            def settle():
                pool.sem_inc(settled, 1)

            def pick_ids(T):
                settle()
                pool.tensor_copy(idx[:, :], ids_sb[:, bass.ds(T, 1), :].rearrange("p a f -> p (a f)"))\
                    .then_inc(idx_ready, 1)
                pool.wait_ge(idx_ready, T + 3)
                settle()

            def gather(f):
                pool.indirect_dma_start(emb[:, f, :], None, tables[f],
                                        bass.IndirectOffsetOnAxis(ap=idx[:, f:f + 1], axis=0)).then_inc(gathered, 16)

            def split_emb(T):
                pool.wait_ge(gathered, (T + 1) * (16 * NF))
                settle()
                src = emb[:, :, :].rearrange("p f d -> p d f")
                pool.tensor_copy(emb2[:, :, 0, :].bitcast(F32R), src).then_inc(high_done, 1)
                pool.wait_ge(high_done, T + 1)
                pool.tensor_tensor(emb2[:, :, 1, :].bitcast(F32R), src, emb2[:, :, 0, :], ALU.subtract)\
                    .then_inc(emb2_ready, 1)

            def fold(n, layer, T, q):
                rows, col = {0: (slice(0, K1), 0), 1: (slice(K1, S), 0), 2: (slice(0, S), 1)}[layer]
                pool.wait_ge(z_read, Z_CREDIT + n + 1)
                r = direct[rows, layer]
                h = half[rows]
                f = feat[rows, col, bass.ds(T * TB, TB)]
                pool.tensor_tensor(h, r[:, 0:2], r[:, 2:4], ALU.add).then_inc(folds, 1)
                pool.wait_ge(folds, FOLD_CREDIT + 3 * n + 1)
                settle()
                if q == 0:
                    pool.tensor_tensor(f, h[:, 0], h[:, 1], ALU.add).then_inc(folds, 2)
                else:
                    pool.tensor_tensor(f, f, h[:, 0], ALU.add).then_inc(folds, 1)
                    pool.wait_ge(folds, FOLD_CREDIT + 3 * n + 2)
                    settle()
                    pool.tensor_tensor(f, f, h[:, 1], ALU.add).then_inc(folds, 1)
                pool.wait_ge(folds, FOLD_CREDIT + 3 * n + 3)
                settle()

            pick_ids(0)
            for f in range(NF):
                gather(f)
            split_emb(0)
            for g in range(2):
                fold(g, 0, 0, g)

            def tile(T, first=False, last=False):
                if not last:
                    pool.wait_ge(emb2_ready, T + 1)
                    pick_ids(T + 1)
                G = T * PER["group"] + 1
                for c in range(CPT):
                    skipped = int(last and c == CPT - 1)
                    if not (first and c == 0):
                        fold(G + group_no(c, 2, skipped), 2, T - (c == 0), (c - 1) % CPT)
                    if not last and c < 2:
                        for f in range(20 * c, min(20 * c + 20, NF)):
                            gather(f)
                        pool.wait_ge(gathered, 16 * (NF * (T + 1) + min(20 * c + 20, NF)))
                    fold(G + group_no(c, 1, skipped), 1, T, c)
                    if not last and c == 1:
                        pool.wait_ge(aux_ready, T * PER["aux"] + AUX * (c + 2) + 1)
                        split_emb(T + 1)
                    if not (last and c >= 2):
                        fold(G + group_no(c, 0), 0, T + (c + 2) // CPT, (c + 2) % CPT)

            tile(0, first=True)
            with pool.Fori(1, TILES - 1) as T:
                tile(T)
            tile(TILES - 1, last=True)
            fold(TILES * PER["group"] - 1, 2, TILES - 1, CPT - 1)

        @block.scalar
        def _(act):
            act.wait_ge(weights_in, 16 * n_loads)
            act.activation(sel0[:, :, :], sel0_st, ACT.Copy).then_inc(parts_made, 1)
            act.activation(sel1[:, :, :], sel1_st, ACT.Copy).then_inc(parts_made, 1)
            act.activation(wh[:, :, :, :], w_st, ACT.Copy).then_inc(parts_made, 1)
            act.activation(half[0:1, 0, 0:1], bias[0:1, 0:1], ACT.Copy).then_inc(z_read, Z_CREDIT)

            def copy_x2(number, slot):
                act.wait_ge(aux_ready, number + 1)
                act.activation(x2[:, slot, :], aux_ps[0:R2, :], ACT.Copy).then_inc(aux_read, 1)

            def square(number, t):
                rows = LAST0 if t == T0 - 1 else R0
                act.wait_ge(aux_ready, number + 1)
                act.activation(sq[0:rows, t % 2, :], aux_ps[0:rows, :], ACT.Square).then_inc(aux_read, 1)

            def copy_xb(T, v, slot):
                act.wait_ge(sel_ready, T * PER["sel"] + v + 1)
                act.activation(xb[:, slot], xb_ps[:, v % 2], ACT.Copy).then_inc(xb_copied, 1)

            def round_(T, s):
                act.wait_ge(products, T * PER["step"] + s + 1 + CREDIT)
                act.activation(Ph[:, s % RING], P[:, s % RING], ACT.Copy).then_inc(rounded, 1)

            def relu(layer, chunk, n, before, z):
                lo, hi = slice(0, K1), slice(K1, S)
                b = bias[:, layer:layer + 1]
                if layer < 2:
                    xk, ready = ((xk1[:, chunk % 2], xk1_ready), (xk2, xk2_ready))[layer]
                    act.activation(xk[lo, :], z[lo], ACT.Relu, bias=b[lo])
                    act.activation(xk[hi, :], z[lo], ACT.Relu, bias=b[lo]).then_inc(ready, 1)
                rows_in = slice(0, S) if layer == 2 else hi
                rows_out = (lo, hi, slice(0, S))[layer]
                act.wait_ge(folds, FOLD_CREDIT + (3 * before + 1 if before is not None else 0))
                act.activation(direct[rows_out, layer].rearrange("p d b -> p (d b)"), z[rows_in], ACT.Relu,
                               bias=b[rows_in]).then_inc(z_read, 1)

            act.wait_ge(weights_made, 4)
            for g in range(2):
                copy_x2(AUX * g, g)
                for t in range(T0):
                    square(AUX * g + 1 + t, t)
                for v in (0, 1) if g == 0 else range(2, PRE):
                    copy_xb(0, v, v)
                act.wait_ge(squares_done, g + 1)
                relu(0, g, g, g - 1 if g else None, z0_ps)
            for s in range(PRE):
                if s < COPY_AHEAD:
                    copy_xb(0, PRE + s, x_slot(0, PRE + s))
                if L1B + s in SPLIT:
                    round_(0, s)

            def tile(T, first=False, last=False):
                G = T * PER["group"] + 1
                for c in range(CPT):
                    end = last and c == CPT - 1
                    no0 = last and c >= 2
                    skipped = int(end)
                    for k in range(STEPS):
                        v = k + COPY_AHEAD
                        if v < PAIRS and not (end and v >= L1B):
                            if v < L1B:
                                act.wait_ge(products, T * PER["step"] + step_no(c - 1, L2 + PRE + v) + 1 + CREDIT)
                                copy_xb(T, PRE + PAIRS * c + v, x_slot(c, PRE + v))
                            else:
                                copy_xb(T, PRE + PAIRS * c + v, x_slot(c + 1, v - L1B))
                        if v >= STEPS and not end:
                            v -= STEPS
                            act.wait_ge(products, T * PER["step"] + step_no(c, L2 + PRE + v) + 1 + CREDIT)
                            copy_xb(T, PRE + PAIRS * (c + 1) + v, x_slot(c + 1, PRE + v))
                        aux = T * PER["aux"] + AUX * (c + 2)
                        if k == X2_AT and not no0:
                            copy_x2(aux, c % 2)
                        if k - SQUARE_LAG in SUM_AT and not no0:
                            t = SUM_AT.index(k - SQUARE_LAG)
                            square(aux + 1 + t, t)
                        if k == RELU2_AT and not (first and c == 0):
                            act.wait_ge(steps_done, T * PER["step"] + step_no(c - 1, STEPS - 1) + 1)
                            n = G + group_no(c, 2, skipped)
                            relu(2, c - 1, n, None if first and c == 1 else n - 3 + skipped, z_ps[:, (c - 1) % 2])
                        if k == RELU1_AT:
                            act.wait_ge(steps_done, T * PER["step"] + step_no(c, L1B - 1) + 1)
                            n = G + group_no(c, 1, skipped)
                            relu(1, c, n, None if first and c == 0 else n - 3 + skipped, z_ps[:, c % 2])
                        if k in SPLIT and not (end and L1B <= k < L2):
                            round_(T, step_no(c, k, end))
                        if k == RELU0_AT and not no0:
                            act.wait_ge(squares_done, T * CPT + c + 3)
                            n = G + group_no(c, 0)
                            relu(0, c + 2, n, n - (2 if first and c == 0 else 3), z0_ps)

            tile(0, first=True)
            with act.Fori(1, TILES - 1) as T:
                tile(T)
            tile(TILES - 1, last=True)
            act.wait_ge(steps_done, all_steps)
            n = TILES * PER["group"] - 1
            relu(2, CPT - 1, n, n - 2, z_ps[:, (CPT - 1) % 2])

            for s in range(BATCH // N + 2):
                if s < BATCH // N:
                    for m in range(H1 // 128):
                        act.wait_ge(m1_ready, 4 * s + m + 1)
                        if s >= 2:
                            act.wait_ge(m2_ready, 2 * (s - 1))
                        act.activation(h1[:, s % 2, m, :], xb_ps[:, m // 2, m % 2, :], ACT.Relu,
                                       bias=bt1[:, m:m + 1]).then_inc(m1_read, 1)
                if 1 <= s <= BATCH // N:
                    for m in range(H2 // 128):
                        act.wait_ge(m2_ready, 2 * (s - 1) + m + 1)
                        if s >= 3:
                            act.wait_ge(m3_ready, s - 2)
                        act.activation(h2[:, (s - 1) % 2, m, :], z_ps[:, m, :], ACT.Relu,
                                       bias=bt2[:, m:m + 1]).then_inc(m2_read, 1)
                if s >= 2:
                    act.wait_ge(m3_ready, s - 1)
                    act.activation(y_sb[0:1, (s - 2) * N:(s - 1) * N], aux_ps[0:1, :], ACT.Copy).then_inc(m3_read, 1)

        @block.vector
        def _(dve):
            dve.memset(half[:, 1, 0:1], 0.0).then_inc(products, CREDIT)
            dve.wait_ge(weights_in, 16 * n_loads)
            dve.tensor_tensor(w0a_st, w0a_st, w0b_st, ALU.add).then_inc(weights_made, 1)
            dve.wait_ge(weights_made, 1)
            dve.tensor_scalar(w0[:, :, :], w0a_st, 0.5, None, ALU.mult).then_inc(weights_made, 1)
            dve.wait_ge(parts_made, 3)
            dve.tensor_tensor(wl[:, :, :, :], w_st, wh[:, :, :, :], ALU.subtract).then_inc(weights_made, 1)
            dve.wait_ge(incident, 1)
            dve.wait_ge(weights_made, 2)
            dve.scalar_tensor_tensor(out=w0[0:NF, 0, :], in0=aux_ps[0:NF, 0:S], scalar=-0.5, in1=w0a_st[0:NF, 0, :],
                                     op0=ALU.mult, op1=ALU.add).then_inc(weights_made, 1)

            def product(T, s, slot, xk):
                dve.tensor_tensor(P[:, s % RING], xb[:, slot], xk.unsqueeze(1).broadcast_to([128, 2, N]), ALU.mult)\
                    .then_inc(products, 1)

            def low(T, s, count):
                dve.wait_ge(rounded, T * PER["split"] + count)
                dve.tensor_tensor(Pl[:, s % RING], P[:, s % RING], Ph[:, s % RING], ALU.subtract)\
                    .then_inc(low_ready, 1)

            dve.wait_ge(xk1_ready, 1)
            for s in range(PRE):
                dve.wait_ge(xb_copied, s + 1)
                product(0, s, s, xk1[:, 0])
                if s and L1B + s - 1 in SPLIT:
                    low(0, s - 1, sum(L1B <= q < L1B + s for q in SPL))
            if L2 - 1 in SPLIT:
                low(0, PRE - 1, NS_PRE)

            def tile(T, last=False):
                for c in range(CPT):
                    end = last and c == CPT - 1
                    waiting = None
                    for k in range(STEPS):
                        if end and L1B <= k < L2:
                            if waiting:
                                low(T, *waiting)
                                waiting = None
                            continue
                        s = step_no(c, k, end)
                        if k == L1B:
                            dve.wait_ge(xk1_ready, T * CPT + c + 2)
                        if k == L2:
                            dve.wait_ge(xk2_ready, T * CPT + c + 1)
                        if k < L2:
                            dve.wait_ge(xb_copied, T * PER["sel"] + PRE + PAIRS * c + k + 1)
                        dve.wait_ge(steps_done, T * PER["step"] + s - RING + 1)
                        if k < L1B:
                            product(T, s, x_slot(c, PRE + k), xk1[:, c % 2])
                        elif k < L2:
                            product(T, s, x_slot(c + 1, k - L1B), xk1[:, (c + 1) % 2])
                        else:
                            product(T, s, x_slot(c, k - L2), xk2[:, :])
                        if waiting:
                            low(T, *waiting)
                        waiting = (s, splits_to(c, k, end)) if k in SPLIT else None
                    if waiting:
                        low(T, *waiting)

            with dve.Fori(0, TILES - 1) as T:
                tile(T)
            tile(TILES - 1, last=True)

        @block.tensor
        def _(pe):
            def transposes(quarter):
                for d in range(DC):
                    m = pe.transpose(aux_ps[0:R2, d * TB:(d + 1) * TB],
                                     emb2[:, quarter * DC + d, :, :].rearrange("p a f -> p (a f)"), ident[:, :])
                m.then_inc(aux_ready, 1)

            def sums(t, slot):
                rows = LAST0 if t == T0 - 1 else R0
                pe.matmul(aux_ps[0:rows, :], sel0[:, t, 0:rows], x2[:, slot, :], start=True, stop=True)\
                    .then_inc(aux_ready, 1)

            def contract0(t):
                rows = LAST0 if t == T0 - 1 else R0
                m = pe.matmul(z0_ps[:, :], w0[0:rows, t, :], sq[0:rows, t % 2, :], start=t == 0, stop=t == T0 - 1)
                if t == T0 - 1:
                    m.then_inc(squares_done, 1)

            def select(v, p, slot):
                for j in range(2):
                    m = pe.matmul(xb_ps[:, v % 2, j, :], sel1[:, 2 * p + j, :], x2[:, slot, :], start=True, stop=True)
                m.then_inc(sel_ready, 1)

            def contract(T, s, k, count, z, start, stop):
                if k not in SPLIT:
                    pe.wait_ge(products, T * PER["step"] + s + 1 + CREDIT)
                    for j in range(2):
                        m = pe.matmul(z, wp[:, PLAIN.index(k), j, :], P[:, s % RING, j, :], start=start and j == 0,
                                      stop=stop and j == 1)
                else:
                    q = SPL.index(k)
                    pe.wait_ge(rounded, T * PER["split"] + count)
                    for j in range(2):
                        for i, w in enumerate((wh, wl)):
                            pe.matmul(z, w[:, q, j, :], Ph[:, s % RING, j, :], start=start and i + j == 0, stop=False)
                    pe.wait_ge(low_ready, T * PER["split"] + count)
                    for j in range(2):
                        m = pe.matmul(z, wh[:, q, j, :], Pl[:, s % RING, j, :], start=False, stop=stop and j == 1)
                m.then_inc(steps_done, 1)

            pe.wait_ge(weights_in, 16 * n_loads)
            pe.wait_ge(weights_made, 1)
            for t in range(T0):
                m = pe.matmul(aux_ps[0:NF, 0:S], inc[:, t, :], w0a_st[:, t, :], start=t == 0, stop=t == T0 - 1)
            m.then_inc(incident, 1)

            pe.wait_ge(weights_made, 4)
            pe.wait_ge(parts_made, 2)
            pe.wait_ge(idx_ready, 2)
            pe.wait_ge(emb2_ready, 1)
            for g in range(2):
                if g:
                    pe.wait_ge(aux_read, AUX * g)
                transposes(g)
                for t in range(T0):
                    pe.wait_ge(aux_read, AUX * g + 1 + t)
                    sums(t, g)
                    if t:
                        if t == 1:
                            pe.wait_ge(z_read, Z_CREDIT + g)
                        contract0(t - 1)
                pe.wait_ge(aux_read, AUX * (g + 1))
                contract0(T0 - 1)
                for v in (0, 1) if g == 0 else range(2, PRE):
                    if v >= 2:
                        pe.wait_ge(xb_copied, v - 1)
                    select(v, v, 0)
            for s in range(-2, PRE):
                v = s + SEL_AHEAD
                pe.wait_ge(xb_copied, v - 1)
                select(v, v, 0)
                if s >= 0:
                    contract(0, s, L1B + s, sum(L1B <= q <= L1B + s for q in SPL), z_ps[:, 0, :], s == 0, False)

            def tile(T, first=False, last=False):
                G = T * PER["group"] + 1
                for c in range(CPT):
                    end = last and c == CPT - 1
                    no0 = last and c >= 2
                    skipped = int(end)
                    z = z_ps[:, c % 2, :]
                    for k in range(STEPS):
                        v = k + SEL_AHEAD
                        cv = c
                        if v >= STEPS:
                            v, cv = v - STEPS, c + 1
                        if v < PAIRS and not (end and (cv > c or v >= L1B)):
                            n = PRE + PAIRS * cv + v
                            pe.wait_ge(xb_copied, T * PER["sel"] + n - 1)
                            if v < L1B:
                                select(n, PRE + v, cv % 2)
                            else:
                                select(n, v - L1B, (cv + 1) % 2)
                        aux = T * PER["aux"] + AUX * (c + 2)
                        if k == TRANSPOSE_AT and not no0:
                            pe.wait_ge(emb2_ready, T + 1 + (c + 2) // CPT)
                            pe.wait_ge(aux_read, aux)
                            transposes((c + 2) % CPT)
                        if k - CONTRACT_LAG in SUM_AT and not no0:
                            t = SUM_AT.index(k - CONTRACT_LAG)
                            if t == 0:
                                n = G + group_no(c - 1, 0) if not (first and c == 0) else 1
                                pe.wait_ge(z_read, Z_CREDIT + n + 1)
                            pe.wait_ge(aux_read, aux + 2 + t)
                            contract0(t)
                        if k in SUM_AT and not no0:
                            t = SUM_AT.index(k)
                            pe.wait_ge(aux_read, aux + 1 + t)
                            sums(t, c % 2)
                        if end and L1B <= k < L2:
                            continue
                        if k == L1B and not (first and c == 0):
                            pe.wait_ge(z_read, Z_CREDIT + G + group_no(c, 2) + 1)
                        if k == L2:
                            pe.wait_ge(z_read, Z_CREDIT + G + group_no(c, 1, skipped) + 1)
                        contract(T, step_no(c, k, end), k, splits_to(c, k, end),
                                 z_ps[:, (c + 1) % 2, :] if L1B <= k < L2 else z, k in (L1B, L2), k in (L1B - 1, STEPS - 1))

            tile(0, first=True)
            with pe.Fori(1, TILES - 1) as T:
                tile(T)
            tile(TILES - 1, last=True)

            groups = TILES * PER["group"]
            pe.wait_ge(z_read, Z_CREDIT + groups)
            pe.wait_ge(folds, FOLD_CREDIT + 3 * groups)
            pe.wait_ge(mlp_in, 3 * 16)
            for s in range(BATCH // N + 2):
                if s < BATCH // N:
                    cols = slice(s * N, (s + 1) * N)
                    for m in range(H1 // 128):
                        if s:
                            pe.wait_ge(m1_read, 4 * (s - 1) + m + 1)
                        o_ = xb_ps[:, m // 2, m % 2, :]
                        for t in range(2):
                            pe.matmul(o_, wt1[:, t, m * 128:(m + 1) * 128], feat[:, t, cols], start=t == 0, stop=False)
                        if s == 0 and m == 0:
                            pe.wait_ge(dense_in, 16)
                        pe.matmul(o_, wt1d[:, m * 128:(m + 1) * 128], dense[:, cols], start=False, stop=True)\
                            .then_inc(m1_ready, 1)
                if 1 <= s <= BATCH // N:
                    pe.wait_ge(m1_read, 4 * s)
                    for m in range(H2 // 128):
                        if s >= 2:
                            pe.wait_ge(m2_read, 2 * (s - 2) + m + 1)
                        for t in range(H1 // 128):
                            i = pe.matmul(z_ps[:, m, :], wt2[:, t, m * 128:(m + 1) * 128], h1[:, (s - 1) % 2, t, :],
                                          start=t == 0, stop=t == H1 // 128 - 1)
                        i.then_inc(m2_ready, 1)
                if s >= 2:
                    pe.wait_ge(m2_read, 2 * (s - 1))
                    if s >= 3:
                        pe.wait_ge(m3_read, s - 2)
                    for t in range(H2 // 128):
                        i = pe.matmul(aux_ps[0:1, :], wt3[:, t:t + 1], h2[:, (s - 2) % 2, t, :],
                                      start=t == 0, stop=t == H2 // 128 - 1)
                    i.then_inc(m3_ready, 1)


def kernel(**inputs):
    import numpy as np
    import concourse.bacc as bacc
    from concourse.bass_utils import run_bass_kernel_spmd

    a = {k: np.ascontiguousarray(v) for k, v in inputs.items()}
    i = np.arange(NF)
    sel0 = np.zeros((2, NF, T0, NO, NF), np.float32)
    inc = np.zeros((NO, NF, T0, NF), np.float32)
    sel1 = np.zeros((2, NF, T1, 2, K1), np.float32)
    w = a["L0_rec_w0"]
    w0a = np.zeros((NO, NF, T0, S), w.dtype)
    w0b = np.zeros((NO, NF, T0, S), w.dtype)
    for t in range(T0):
        for r in range(NO):
            offset = NO * t + r
            if offset > NF // 2:
                continue
            j = (i + offset) % NF
            sel0[:, i, t, r, i] = 1
            sel0[:, j, t, r, i] = 1
            w0a[r, :, t] = w[i, j]
            if offset:
                w0b[r, :, t] = w[j, i]
                inc[r, i, t, i] = 1
                inc[r, i, t, j] = 1
    for t in range(T1):
        for j in range(2):
            sel1[:, min(2 * t + j, NF - 1), t, j] = 1

    def tiled(w):
        p = np.zeros((2 * T1, K1, S), w.dtype)
        p[:NF] = w
        return np.ascontiguousarray(p.reshape(T1, 2 * K1, S).transpose(1, 0, 2))

    arrays = {
        "ids": a["ids"],
        "sel0": sel0.reshape(R2, T0, R0), "sel1": sel1.reshape(R2, T1, 128), "inc": inc.reshape(R0, T0, NF),
        "w0a": w0a.reshape(R0, T0, S), "w0b": w0b.reshape(R0, T0, S),
        "w1": tiled(a["L0_rec_w1"]), "w2": tiled(a["L0_rec_w2"]),
        "b": np.ascontiguousarray(np.stack([a["L0_rec_b0"], a["L0_rec_b1"], a["L0_rec_b2"]], axis=1)),
        "dense": np.ascontiguousarray(a["dense_ctx"].T),
        "wt1": a["W_top1"], "bt1": np.ascontiguousarray(a["b_top1"].reshape(H1 // 128, 128).T),
        "wt2": a["W_top2"], "bt2": np.ascontiguousarray(a["b_top2"].reshape(H2 // 128, 128).T),
        "wt3": np.ascontiguousarray(a["W_top3"].reshape(H2 // 128, 128).T),
    }
    names = list(arrays)
    for f in range(NF):
        arrays[f"tbl_{f}"] = a[f"tbl_{f}"]
    nc = bacc.Bacc("TRN2", target_bir_lowering=False, num_devices=1)
    ap = {k: nc.dram_tensor(f"{k}_in", v.shape, mybir.dt.from_np(v.dtype), kind="ExternalInput").ap()
          for k, v in arrays.items()}
    out = nc.dram_tensor("y_out", (BATCH, 1), F32, kind="ExternalOutput").ap()
    build(nc, ap["ids"], [ap[f"tbl_{f}"] for f in range(NF)], *[ap[k] for k in names[1:]], out)
    return run_bass_kernel_spmd(nc, [{f"{k}_in": v for k, v in arrays.items()}], core_ids=[0]).results[0]["y_out"]
```

```python
import concourse.bass as bass
from concourse import mybir
from contextlib import ExitStack

F32 = mybir.dt.float32
F32R = mybir.dt.float32r
I32 = mybir.dt.int32
ALU = mybir.AluOpType
ACT = mybir.ActivationFunctionType

BATCH, NF, D, S, K1 = 2048, 39, 16, 128, 64
DENSE, H1, H2 = 16, 512, 256
GAP = 32
DX = 3 * GAP
TB = 128
TILES = BATCH // TB
DC = 4
CPT = D // DC
N = DC * TB
R2 = 2 * NF
NO = 3
R0 = NO * NF
T0 = 7
LAST0 = 2 * NF
T1 = 20
PAIRS = T1 // 2

PRE = 4
L1B, L2, STEPS = PAIRS - PRE, PAIRS, 2 * PAIRS
SPLIT = {0, 2, 5, 6, 7, 8, 10, 13, 14, 15, 17, 18}
RING = 4
XSLOTS = PAIRS + PRE
TRANSPOSE_AT, X2_AT = 0, 1
ROWS_AT, ROWS_COPY_AT = 2, 3
SUM_AT = [3, 5, 7, 9, 11, 12, 14]
SQUARE_LAG, CONTRACT_LAG = 2, 3
RELU2_AT, RELU1_AT, RELU0_AT = 3, 9, 19
SPL = sorted(SPLIT)
PLAIN = [k for k in range(STEPS) if k not in SPLIT]
NS, NS_PRE = len(SPL), sum(L1B <= k < L2 for k in SPL)
CREDIT = 2
FOLD_CREDIT = 9
Z_CREDIT = 1
AUX = 2 + T0
SCRATCH = 4
SINGLE = 2 * PRE + 1
SINGLE_STEPS = [k for k in range(STEPS) if (k + PRE if k < L1B else k - L1B if k < L2 else k - L2) == SINGLE // 2]
assert all(k in SPLIT for k in SINGLE_STEPS)

PER = dict(step=STEPS * CPT, split=NS * CPT, group=3 * CPT, aux=AUX * CPT)


def step_no(c, k, end=False):
    return PRE + STEPS * c + k - (PRE if end and k >= L2 else 0)


def splits_to(c, k, end=False):
    return NS_PRE + NS * c + sum(s <= k for s in SPL) - (NS_PRE if end and k >= L2 else 0)


def group_no(c, layer, skipped=0):
    return 3 * c + {2: 0, 1: 1, 0: 2}[layer] - skipped


def x_slot(chunk, p):
    return PRE * (chunk % 2) + p if p < PRE else PRE + p


def field(t, j):
    return NF - 1 if t == SINGLE else 2 * t + j - (2 if t > SINGLE else 0)


def fills(T, c, p):
    return 2 * T + c // 2 + 1 if p < PRE else CPT * T + c + 1


def build(nc, ids, tables, x0_dram, sel0_d, inc_d, w0a_d, w0b_d, w1_d, w2_d, b_d, dense_d, wt1_d, wx_d, bt1_d, wt2_d, bt2_d,
          wt3_d, out):
    ctx = ExitStack()
    with ctx:
        def sb(name, shape, dt=F32):
            return ctx.enter_context(nc.sbuf_tensor(name, shape, dt))

        def pb(name, shape):
            return ctx.enter_context(nc.psum_tensor(name, shape, F32))

        def sem(name):
            return ctx.enter_context(nc.semaphore(name))

        ids_sb = sb("ids_sb", [TB, TILES, NF], I32)
        idx = sb("idx", [TB, NF], I32)
        emb = sb("emb", [TB, NF, D])
        emb2 = sb("emb2", [TB, D, 2, NF])
        x2 = sb("x2", [R2, 2, N], F32R)
        sel0 = sb("sel0", [R2, T0 + 1, R0], F32R)
        rows_sb = sb("rows_sb", [NF, 2, N])
        sq = sb("sq", [R0, 2, N])
        xb = sb("xb", [128, XSLOTS, 2, N])
        xk1 = sb("xk1", [128, 2, N])
        xk2 = sb("xk2", [128, N])
        P = sb("P", [128, RING, 2, N])
        Ph = sb("Ph", [128, RING, 2, N], F32R)
        Pl = sb("Pl", [128, RING, 2, N], F32R)
        w0 = sb("w0", [R0, T0, S])
        wp = sb("wp", [128, len(PLAIN), 2, S])
        wh = sb("wh", [128, NS, 2, S], F32R)
        wl = sb("wl", [128, NS, 2, S], F32R)
        bias = sb("bias", [S, 3])
        direct = sb("direct", [128, 3, DC, TB])
        half = sb("half", [128, 2, TB])
        feat = sb("feat", [128, 2, BATCH])
        ident = sb("ident", [128, 128])
        dense = sb("dense", [DX, BATCH], F32R)
        wt3 = sb("wt3", [128, H2 // 128])
        bt1 = sb("bt1", [128, H1 // 128])
        bt2 = sb("bt2", [128, H2 // 128])
        xflat = xb[:, :, :, :].rearrange("p q j n -> p (q j n)")
        at = [0]

        def stage(rows, a, b):
            at[0] += a * b
            return xflat[0:rows, at[0] - a * b:at[0]].rearrange("p (a b) -> p a b", b=b)

        sel0_st, inc = stage(R2, T0 + 1, R0), stage(R0, T0, NF)
        w0a_st, w0b_st = stage(R0, T0, S), stage(R0, T0, S)
        w_st = stage(128, NS, 2 * S).rearrange("p q (j m) -> p q j m", j=2)
        xt = xb[:, :, :, :].rearrange("p q j n -> p (q j) n")
        wt1 = xt[:, 0:2, :]
        wt2 = xt[:, 2:4, :].rearrange("p a (b n) -> p (a b) n", n=H2)
        wx_st = xt[0:DX, 4, :]
        dense_st = xt[0:DX, 8:12, :].rearrange("p t n -> p (t n)")
        y_sb = xt[0:1, 12:16, :].rearrange("p t n -> p (t n)")
        h1 = xt[:, 16:24, :].rearrange("p (u m) n -> p u m n", u=2)
        h2 = xt[:, 24:28, :].rearrange("p (u m) n -> p u m n", u=2)
        assert SPL[5] < L2
        wt1h, wt1l = (v[:, 0:4].rearrange("p q j m -> p (q j m)").rearrange("p (t n) -> p t n", n=H1)
                      for v in (wh, wl))
        wx = wh[0:DX, 4:6].rearrange("p q j m -> p (q j m)")

        ps = pb("ps", [128, 8, N])
        z_ps = ps[:, 0:2, :]
        z0_ps = ps[:, 2, :]
        aux_ps = ps[:, 3:5, :]
        m1_ps, m2_ps, m3_ps = ps[:, 4:8, :], ps[:, 0:2, :], ps[:, 3, :]

        ids_in = sem("ids_in")
        weights_in = sem("weights_in")
        parts_made = sem("parts_made")
        weights_made = sem("weights_made")
        incident = sem("incident")
        idx_ready = sem("idx_ready")
        gathered = sem("gathered")
        high_done = sem("high_done")
        emb2_ready = sem("emb2_ready")
        settled = sem("settled")
        aux_ready = sem("aux_ready")
        aux_read = sem("aux_read")
        rows_written = sem("rows_written")
        rows_settled = sem("rows_settled")
        xb_in = [sem(f"xb_in_{q}") for q in range(XSLOTS)]
        products = sem("products")
        rounded = sem("rounded")
        low_ready = sem("low_ready")
        steps_done = sem("steps_done")
        squares_done = sem("squares_done")
        xk1_ready = sem("xk1_ready")
        xk2_ready = sem("xk2_ready")
        z_read = sem("z_read")
        folds = sem("folds")
        dense_in = sem("dense_in")
        mlp_in = sem("mlp_in")
        mlp_high = sem("mlp_high")
        mlp_low = sem("mlp_low")
        dense_high = sem("dense_high")
        dense_low = sem("dense_low")
        feat_high = sem("feat_high")
        feat_low = sem("feat_low")
        m1_ready = sem("m1_ready")
        m1_read = sem("m1_read")
        m2_ready = sem("m2_ready")
        m2_read = sem("m2_read")
        m3_ready = sem("m3_ready")
        m3_read = sem("m3_read")
        out_done = sem("out_done")

        block = ctx.enter_context(nc.Block())

        def dram_pair(k):
            if k >= L2:
                return w2_d[:, 2 * (k - L2):2 * (k - L2) + 2, :]
            p = (k + PRE) % PAIRS
            return w1_d[:, 2 * p:2 * p + 2, :]

        n_loads = 8 + STEPS
        all_steps = TILES * PER["step"]
        groups = TILES * PER["group"]
        blocks = BATCH // N

        def folds_for(s):
            tiles = (s + 1) * N // TB
            return FOLD_CREDIT + 3 * min(tiles * PER["group"] + 2, groups)

        def ring_left(s):
            return all_steps - RING + 1 + s

        def feat_block(s):
            return feat[:, :, s * N:(s + 1) * N]

        @block.sync
        def _(sp):
            sp.dma_start(ids_sb[:, :, :], ids.rearrange("(t p) f -> p t f", p=TB)).then_inc(ids_in, 16)
            for dst, src in ((w0a_st, w0a_d), (w0b_st, w0b_d), (inc, inc_d), (sel0_st, sel0_d),
                             (bias[:, :], b_d), (wt3[:, :], wt3_d), (bt1[:, :], bt1_d), (bt2[:, :], bt2_d)):
                sp.dma_start(dst, src).then_inc(weights_in, 16)
            for q, k in enumerate(SPL):
                sp.dma_start(w_st[:, q], dram_pair(k)).then_inc(weights_in, 16)
            for q, k in enumerate(PLAIN):
                sp.dma_start(wp[:, q], dram_pair(k)).then_inc(weights_in, 16)

            def write_rows(T, c):
                sp.wait_ge(aux_read, T * PER["aux"] + AUX * c + 2)
                sp.dma_start(x0_dram[c % SCRATCH, 0:NF, :], rows_sb[:, c % 2, :]).then_inc(rows_written, 16)
                sp.wait_ge(rows_written, 16 * (T * CPT + c + 1))
                sp.sem_inc(rows_settled, 1)

            def spread(c, p):
                q = x_slot(c, p)
                for j in range(2):
                    h, h2 = field(2 * p, j), field(2 * p + 1, j)
                    src = x0_dram[c % SCRATCH, h:h2 + 1:h2 - h, :]
                    sp.dma_start(xb[j * K1:(j + 1) * K1, q, :, :], src.unsqueeze(0).broadcast_to([K1, 2, N]))\
                        .then_inc(xb_in[q], 16)

            sp.wait_ge(weights_made, 6)
            sp.wait_ge(parts_made, 2)
            for c in range(2):
                write_rows(0, c)
                for p in range(PRE if c else PAIRS):
                    spread(c, p)

            def tile(T, last=False):
                for c in range(CPT):
                    if not (last and c >= 2):
                        write_rows(T, c + 2)
                    if last and c == CPT - 1:
                        continue
                    for p in range(PAIRS):
                        if last and c == 2 and p < PRE:
                            continue
                        sp.wait_ge(products, T * PER["step"] + step_no(c, L2 + p) + 1 + CREDIT)
                        spread(c + 2 if p < PRE else c + 1, p)

            with sp.Fori(0, TILES - 1) as T:
                tile(T)
            tile(TILES - 1, last=True)

            sp.wait_ge(products, CREDIT + PRE + all_steps - STEPS)
            sp.dma_start(wt1, wt1_d[0:256, :].rearrange("(t p) n -> p t n", p=128)).then_inc(mlp_in, 16)
            sp.dma_start(wt2, wt2_d.rearrange("(t p) n -> p t n", p=128)).then_inc(mlp_in, 16)
            sp.dma_start(wx_st, wx_d).then_inc(mlp_in, 16)
            sp.wait_ge(products, CREDIT + all_steps - (PAIRS - PRE))
            sp.dma_start(dense_st, dense_d).then_inc(dense_in, 16)
            sp.wait_ge(m3_read, BATCH // N)
            sp.dma_start(out.rearrange("(a n) o -> a (n o)", a=1), y_sb).then_inc(out_done, 16)
            sp.wait_ge(out_done, 16)

        @block.gpsimd
        def _(pool):
            for layer in range(3):
                pool.memset(direct[:, layer], 0.0).then_inc(folds, 3)
            pool.memset(ident[:, :], 0.0).then_inc(idx_ready, 1)
            pool.wait_ge(idx_ready, 1)
            pool.affine_select(out=ident[:, :], in_=ident[:, :], compare_op=ALU.not_equal, fill=1.0, base=0,
                               pattern=[[-1, 128]], channel_multiplier=1).then_inc(idx_ready, 1)
            pool.wait_ge(ids_in, 16)

            def settle():
                pool.sem_inc(settled, 1)

            def pick_ids(T):
                settle()
                pool.tensor_copy(idx[:, :], ids_sb[:, bass.ds(T, 1), :].rearrange("p a f -> p (a f)"))\
                    .then_inc(idx_ready, 1)
                pool.wait_ge(idx_ready, T + 3)
                settle()

            def gather(f):
                pool.indirect_dma_start(emb[:, f, :], None, tables[f],
                                        bass.IndirectOffsetOnAxis(ap=idx[:, f:f + 1], axis=0)).then_inc(gathered, 16)

            def split_emb(T):
                pool.wait_ge(gathered, (T + 1) * (16 * NF))
                settle()
                src = emb[:, :, :].rearrange("p f d -> p d f")
                pool.tensor_copy(emb2[:, :, 0, :].bitcast(F32R), src).then_inc(high_done, 1)
                pool.wait_ge(high_done, T + 1)
                pool.tensor_tensor(emb2[:, :, 1, :].bitcast(F32R), src, emb2[:, :, 0, :], ALU.subtract)\
                    .then_inc(emb2_ready, 1)

            def fold(n, layer, T, q):
                rows, col = {0: (slice(0, K1), 0), 1: (slice(K1, S), 0), 2: (slice(0, S), 1)}[layer]
                pool.wait_ge(z_read, Z_CREDIT + n + 1)
                r = direct[rows, layer]
                h = half[rows]
                f = feat[rows, col, bass.ds(T * TB, TB)]
                pool.tensor_tensor(h, r[:, 0:2], r[:, 2:4], ALU.add).then_inc(folds, 1)
                pool.wait_ge(folds, FOLD_CREDIT + 3 * n + 1)
                settle()
                if q == 0:
                    pool.tensor_tensor(f, h[:, 0], h[:, 1], ALU.add).then_inc(folds, 2)
                else:
                    pool.tensor_tensor(f, f, h[:, 0], ALU.add).then_inc(folds, 1)
                    pool.wait_ge(folds, FOLD_CREDIT + 3 * n + 2)
                    settle()
                    pool.tensor_tensor(f, f, h[:, 1], ALU.add).then_inc(folds, 1)
                pool.wait_ge(folds, FOLD_CREDIT + 3 * n + 3)
                settle()

            pick_ids(0)
            for f in range(NF):
                gather(f)
            split_emb(0)
            for g in range(2):
                fold(g, 0, 0, g)

            def tile(T, first=False, last=False):
                if not last:
                    pool.wait_ge(emb2_ready, T + 1)
                    pick_ids(T + 1)
                G = T * PER["group"] + 1
                for c in range(CPT):
                    skipped = int(last and c == CPT - 1)
                    if not (first and c == 0):
                        fold(G + group_no(c, 2, skipped), 2, T - (c == 0), (c - 1) % CPT)
                    if not last and c < 2:
                        for f in range(20 * c, min(20 * c + 20, NF)):
                            gather(f)
                        pool.wait_ge(gathered, 16 * (NF * (T + 1) + min(20 * c + 20, NF)))
                    fold(G + group_no(c, 1, skipped), 1, T, c)
                    if not last and c == 1:
                        pool.wait_ge(aux_ready, T * PER["aux"] + AUX * (c + 2) + 1)
                        split_emb(T + 1)
                    if not (last and c >= 2):
                        fold(G + group_no(c, 0), 0, T + (c + 2) // CPT, (c + 2) % CPT)

            tile(0, first=True)
            with pool.Fori(1, TILES - 1) as T:
                tile(T)
            tile(TILES - 1, last=True)
            fold(TILES * PER["group"] - 1, 2, TILES - 1, CPT - 1)

        @block.scalar
        def _(act):
            act.wait_ge(weights_in, 16 * n_loads)
            act.activation(sel0[:, :, :], sel0_st, ACT.Copy).then_inc(parts_made, 1)
            act.activation(wh[:, :, :, :], w_st, ACT.Copy).then_inc(parts_made, 1)
            act.activation(half[0:1, 0, 0:1], bias[0:1, 0:1], ACT.Copy).then_inc(z_read, Z_CREDIT)

            def copy_x2(T, number, slot):
                act.wait_ge(aux_ready, T * PER["aux"] + number + 1)
                act.activation(x2[:, slot, :], aux_ps[0:R2, number % 2, :], ACT.Copy).then_inc(aux_read, 1)

            def copy_rows(T, number, slot):
                act.wait_ge(aux_ready, T * PER["aux"] + number + 1)
                act.activation(rows_sb[:, slot, :], aux_ps[0:NF, number % 2, :], ACT.Copy).then_inc(aux_read, 1)

            def square(T, number, t):
                rows = LAST0 if t == T0 - 1 else R0
                act.wait_ge(aux_ready, T * PER["aux"] + number + 1)
                act.activation(sq[0:rows, t % 2, :], aux_ps[0:rows, number % 2, :], ACT.Square).then_inc(aux_read, 1)

            def round_(T, s):
                act.wait_ge(products, T * PER["step"] + s + 1 + CREDIT)
                act.activation(Ph[:, s % RING], P[:, s % RING], ACT.Copy).then_inc(rounded, 1)

            def relu(layer, chunk, n, before, z):
                lo, hi = slice(0, K1), slice(K1, S)
                b = bias[:, layer:layer + 1]
                if layer < 2:
                    xk, ready = ((xk1[:, chunk % 2], xk1_ready), (xk2, xk2_ready))[layer]
                    act.activation(xk[lo, :], z[lo], ACT.Relu, bias=b[lo])
                    act.activation(xk[hi, :], z[lo], ACT.Relu, bias=b[lo]).then_inc(ready, 1)
                rows_in = slice(0, S) if layer == 2 else hi
                rows_out = (lo, hi, slice(0, S))[layer]
                act.wait_ge(folds, FOLD_CREDIT + (3 * before + 1 if before is not None else 0))
                act.activation(direct[rows_out, layer].rearrange("p d b -> p (d b)"), z[rows_in], ACT.Relu,
                               bias=b[rows_in]).then_inc(z_read, 1)

            for g in range(2):
                copy_x2(0, AUX * g, g)
                copy_rows(0, AUX * g + 1, g)
                for t in range(T0):
                    square(0, AUX * g + 2 + t, t)
                    s = t - (T0 - PRE - 1)
                    if g and 0 <= s < PRE and L1B + s in SPLIT:
                        round_(0, s)
                act.wait_ge(squares_done, g + 1)
                relu(0, g, g, g - 1 if g else None, z0_ps)

            def tile(T, first=False, last=False):
                G = T * PER["group"] + 1
                for c in range(CPT):
                    end = last and c == CPT - 1
                    no0 = last and c >= 2
                    skipped = int(end)
                    for k in range(STEPS):
                        aux = AUX * (c + 2)
                        if k == X2_AT and not no0:
                            copy_x2(T, aux, c % 2)
                        if k == ROWS_COPY_AT and not no0:
                            act.wait_ge(rows_written, 16 * (T * CPT + c + 1))
                            copy_rows(T, aux + 1, c % 2)
                        if k - SQUARE_LAG in SUM_AT and not no0:
                            t = SUM_AT.index(k - SQUARE_LAG)
                            square(T, aux + 2 + t, t)
                        if k == RELU2_AT and not (first and c == 0):
                            act.wait_ge(steps_done, T * PER["step"] + step_no(c - 1, STEPS - 1) + 1)
                            n = G + group_no(c, 2, skipped)
                            relu(2, c - 1, n, None if first and c == 1 else n - 3 + skipped, z_ps[:, (c - 1) % 2])
                        if k == RELU1_AT:
                            act.wait_ge(steps_done, T * PER["step"] + step_no(c, L1B - 1) + 1)
                            n = G + group_no(c, 1, skipped)
                            relu(1, c, n, None if first and c == 0 else n - 3 + skipped, z_ps[:, c % 2])
                        if k in SPLIT and not (end and L1B <= k < L2):
                            round_(T, step_no(c, k, end))
                        if end and k == L2 + 3:
                            act.wait_ge(mlp_in, 3 * 16)
                            act.wait_ge(steps_done, all_steps - PAIRS)
                            act.activation(wt1h, wt1, ACT.Copy).then_inc(mlp_high, 1)
                            act.activation(wx, wx_st, ACT.Copy).then_inc(mlp_high, 1)
                        if end and k == STEPS - 1:
                            act.wait_ge(dense_in, 16)
                            act.activation(dense[:, :], dense_st, ACT.Copy).then_inc(dense_high, 1)
                        if k == RELU0_AT and not no0:
                            act.wait_ge(squares_done, T * CPT + c + 3)
                            n = G + group_no(c, 0)
                            relu(0, c + 2, n, n - (2 if first and c == 0 else 3), z0_ps)

            tile(0, first=True)
            with act.Fori(1, TILES - 1) as T:
                tile(T)
            tile(TILES - 1, last=True)

            def round_feat(s):
                act.wait_ge(folds, folds_for(s))
                act.wait_ge(steps_done, ring_left(s))
                act.activation(Ph[:, s], feat_block(s), ACT.Copy).then_inc(feat_high, 1)

            for s in range(blocks - 1):
                round_feat(s)
            act.wait_ge(steps_done, all_steps)
            relu(2, CPT - 1, groups - 1, groups - 3, z_ps[:, (CPT - 1) % 2])

            for s in range(blocks + 2):
                if s < blocks:
                    for m in range(H1 // 128):
                        act.wait_ge(m1_ready, 4 * s + m + 1)
                        if s >= 2:
                            act.wait_ge(m2_ready, 2 * (s - 1))
                        act.activation(h1[:, s % 2, m, :], m1_ps[:, m, :], ACT.Relu,
                                       bias=bt1[:, m:m + 1]).then_inc(m1_read, 1)
                if s == 1:
                    round_feat(blocks - 1)
                if 1 <= s <= blocks:
                    for m in range(H2 // 128):
                        act.wait_ge(m2_ready, 2 * (s - 1) + m + 1)
                        if s >= 3:
                            act.wait_ge(m3_ready, s - 2)
                        act.activation(h2[:, (s - 1) % 2, m, :], m2_ps[:, m, :], ACT.Relu,
                                       bias=bt2[:, m:m + 1]).then_inc(m2_read, 1)
                if s >= 2:
                    act.wait_ge(m3_ready, s - 1)
                    act.activation(y_sb[:, (s - 2) * N:(s - 1) * N], m3_ps[0:1, :], ACT.Copy).then_inc(m3_read, 1)

        @block.vector
        def _(dve):
            dve.memset(half[:, 1, 0:1], 0.0).then_inc(products, CREDIT)
            dve.wait_ge(weights_in, 16 * n_loads)
            dve.tensor_tensor(w0a_st, w0a_st, w0b_st, ALU.add).then_inc(weights_made, 1)
            dve.wait_ge(weights_made, 1)
            dve.tensor_scalar(w0[:, :, :], w0a_st, 0.5, None, ALU.mult).then_inc(weights_made, 1)
            dve.wait_ge(parts_made, 2)
            dve.tensor_tensor(wl[:, :, :, :], w_st, wh[:, :, :, :], ALU.subtract).then_inc(weights_made, 1)
            dve.wait_ge(weights_made, 3)
            for k in SINGLE_STEPS:
                q = SPL.index(k)
                dve.tensor_copy(wh[K1:, q, 1, :], wl[K1:, q, 1, :]).then_inc(weights_made, 1)
            dve.wait_ge(incident, 1)
            dve.scalar_tensor_tensor(out=w0[0:NF, 0, :], in0=aux_ps[0:NF, 0, 0:S], scalar=-0.5, in1=w0a_st[0:NF, 0, :],
                                     op0=ALU.mult, op1=ALU.add).then_inc(weights_made, 1)

            def product(T, s, slot, xk):
                dve.tensor_tensor(P[:, s % RING], xb[:, slot], xk.unsqueeze(1).broadcast_to([128, 2, N]), ALU.mult)\
                    .then_inc(products, 1)

            def low(T, s, count):
                dve.wait_ge(rounded, T * PER["split"] + count)
                dve.tensor_tensor(Pl[:, s % RING], P[:, s % RING], Ph[:, s % RING], ALU.subtract)\
                    .then_inc(low_ready, 1)

            dve.wait_ge(xk1_ready, 1)
            for s in range(PRE):
                dve.wait_ge(xb_in[s], 32)
                product(0, s, s, xk1[:, 0])
                if s and L1B + s - 1 in SPLIT:
                    low(0, s - 1, sum(L1B <= q < L1B + s for q in SPL))
            if L2 - 1 in SPLIT:
                low(0, PRE - 1, NS_PRE)

            def tile(T, last=False):
                for c in range(CPT):
                    end = last and c == CPT - 1
                    waiting = None
                    for k in range(STEPS):
                        if end and L1B <= k < L2:
                            if waiting:
                                low(T, *waiting)
                                waiting = None
                            continue
                        s = step_no(c, k, end)
                        if k == L1B:
                            dve.wait_ge(xk1_ready, T * CPT + c + 2)
                        if k == L2:
                            dve.wait_ge(xk2_ready, T * CPT + c + 1)
                        if k < L2:
                            ch, p = (c, PRE + k) if k < L1B else (c + 1, k - L1B)
                            dve.wait_ge(xb_in[x_slot(ch, p)], 32 * fills(T, ch, p))
                        dve.wait_ge(steps_done, T * PER["step"] + s - RING + 1)
                        if k < L1B:
                            product(T, s, x_slot(c, PRE + k), xk1[:, c % 2])
                        elif k < L2:
                            product(T, s, x_slot(c + 1, k - L1B), xk1[:, (c + 1) % 2])
                        else:
                            product(T, s, x_slot(c, k - L2), xk2[:, :])
                        if waiting:
                            low(T, *waiting)
                        waiting = (s, splits_to(c, k, end)) if k in SPLIT else None
                        if end and k == L2 + 5:
                            dve.wait_ge(mlp_high, 2)
                            dve.wait_ge(steps_done, all_steps - PAIRS)
                            dve.tensor_tensor(wt1l, wt1, wt1h, ALU.subtract).then_inc(mlp_low, 1)
                            r = slice(2 * GAP, DX)
                            dve.tensor_tensor(wx[r], wx_st[r], wx[r], ALU.subtract).then_inc(mlp_low, 1)
                    if waiting:
                        low(T, *waiting)

            with dve.Fori(0, TILES - 1) as T:
                tile(T)
            tile(TILES - 1, last=True)

            def low_feat(s):
                dve.wait_ge(steps_done, ring_left(s))
                dve.wait_ge(feat_high, s + 1)
                dve.tensor_tensor(Pl[:, s], feat_block(s), Ph[:, s], ALU.subtract).then_inc(feat_low, 1)

            dve.wait_ge(dense_high, 1)
            r = slice(GAP, 2 * GAP)
            dve.tensor_tensor(dense[r], dense_st[r], dense[r], ALU.subtract).then_inc(dense_low, 1)
            for s in range(blocks):
                low_feat(s)

        @block.tensor
        def _(pe):
            def transposes(number, quarter):
                for d in range(DC):
                    m = pe.transpose(aux_ps[0:R2, number % 2, d * TB:(d + 1) * TB],
                                     emb2[:, quarter * DC + d, :, :].rearrange("p a f -> p (a f)"), ident[:, :])
                m.then_inc(aux_ready, 1)

            def sums(number, t, slot):
                rows = LAST0 if t >= T0 - 1 else R0
                pe.matmul(aux_ps[0:rows, number % 2, :], sel0[:, t, 0:rows], x2[:, slot, :], start=True, stop=True)\
                    .then_inc(aux_ready, 1)

            def contract0(t):
                rows = LAST0 if t == T0 - 1 else R0
                m = pe.matmul(z0_ps, w0[0:rows, t, :], sq[0:rows, t % 2, :], start=t == 0, stop=t == T0 - 1)
                if t == T0 - 1:
                    m.then_inc(squares_done, 1)

            def contract(T, s, k, count, z, start, stop):
                if k not in SPLIT:
                    pe.wait_ge(products, T * PER["step"] + s + 1 + CREDIT)
                    for j in range(2):
                        m = pe.matmul(z, wp[:, PLAIN.index(k), j, :], P[:, s % RING, j, :], start=start and j == 0,
                                      stop=stop and j == 1)
                else:
                    q = SPL.index(k)
                    pe.wait_ge(rounded, T * PER["split"] + count)
                    twice = k in SINGLE_STEPS
                    for j in range(2):
                        for i, w in enumerate((wh,) if twice and j else (wh, wl)):
                            pe.matmul(z, w[:, q, j, :], Ph[:, s % RING, j, :], start=start and i + j == 0, stop=False)
                    pe.wait_ge(low_ready, T * PER["split"] + count)
                    for j in range(2):
                        rows = slice(0, K1 if twice and j else 128)
                        m = pe.matmul(z, wh[rows, q, j, :], Pl[rows, s % RING, j, :], start=False,
                                      stop=stop and j == 1)
                m.then_inc(steps_done, 1)

            pe.wait_ge(weights_in, 16 * n_loads)
            pe.wait_ge(weights_made, 1)
            for t in range(T0):
                m = pe.matmul(aux_ps[0:NF, 0, 0:S], inc[:, t, :], w0a_st[:, t, :], start=t == 0, stop=t == T0 - 1)
            m.then_inc(incident, 1)

            pe.wait_ge(weights_made, 6)
            pe.wait_ge(parts_made, 1)
            pe.wait_ge(idx_ready, 2)
            pe.wait_ge(emb2_ready, 1)
            for g in range(2):
                number = AUX * g
                if g:
                    pe.wait_ge(aux_read, number - 1)
                transposes(number, g)
                pe.wait_ge(aux_read, number + 1)
                sums(number + 1, T0, g)
                for t in range(T0):
                    pe.wait_ge(aux_read, number + 1 + t)
                    sums(number + 2 + t, t, g)
                    if t:
                        if t == 1:
                            pe.wait_ge(z_read, Z_CREDIT + g)
                        pe.wait_ge(aux_read, number + 2 + t)
                        contract0(t - 1)
                    if g and t >= T0 - PRE:
                        s = t - (T0 - PRE)
                        contract(0, s, L1B + s, sum(L1B <= q <= L1B + s for q in SPL), z_ps[:, 0, :], s == 0, False)
                pe.wait_ge(aux_read, AUX * (g + 1))
                contract0(T0 - 1)

            def tile(T, first=False, last=False):
                G = T * PER["group"] + 1
                for c in range(CPT):
                    end = last and c == CPT - 1
                    no0 = last and c >= 2
                    skipped = int(end)
                    z = z_ps[:, c % 2, :]
                    for k in range(STEPS):
                        number = AUX * (c + 2)
                        aux = T * PER["aux"] + number
                        if k == TRANSPOSE_AT and not no0:
                            pe.wait_ge(emb2_ready, T + 1 + (c + 2) // CPT)
                            pe.wait_ge(aux_read, aux - 1)
                            transposes(number, (c + 2) % CPT)
                        if k == ROWS_AT and not no0:
                            pe.wait_ge(aux_read, aux + 1)
                            sums(number + 1, T0, c % 2)
                        if k - CONTRACT_LAG in SUM_AT and not no0:
                            t = SUM_AT.index(k - CONTRACT_LAG)
                            if t == 0:
                                n = G + group_no(c - 1, 0) if not (first and c == 0) else 1
                                pe.wait_ge(z_read, Z_CREDIT + n + 1)
                            pe.wait_ge(aux_read, aux + 3 + t)
                            contract0(t)
                        if k in SUM_AT and not no0:
                            t = SUM_AT.index(k)
                            pe.wait_ge(aux_read, aux + 1 + t)
                            sums(number + 2 + t, t, c % 2)
                        if end and L1B <= k < L2:
                            continue
                        if k == L1B and not (first and c == 0):
                            pe.wait_ge(z_read, Z_CREDIT + G + group_no(c, 2) + 1)
                        if k == L2:
                            pe.wait_ge(z_read, Z_CREDIT + G + group_no(c, 1, skipped) + 1)
                        contract(T, step_no(c, k, end), k, splits_to(c, k, end),
                                 z_ps[:, (c + 1) % 2, :] if L1B <= k < L2 else z, k in (L1B, L2), k in (L1B - 1, STEPS - 1))

            tile(0, first=True)
            with pe.Fori(1, TILES - 1) as T:
                tile(T)
            tile(TILES - 1, last=True)

            pe.wait_ge(mlp_low, 2)
            for s in range(blocks + 2):
                if s < blocks:
                    if s == 0:
                        pe.wait_ge(dense_low, 1)
                    pe.wait_ge(feat_low, s + 1)
                    for m in range(H1 // 128):
                        if s:
                            pe.wait_ge(m1_read, 4 * (s - 1) + m + 1)
                        o_, ms = m1_ps[:, m, :], slice(m * 128, (m + 1) * 128)
                        pe.matmul(o_, wx[:, ms], dense[:, s * N:(s + 1) * N], start=True, stop=False)
                        for t in range(2):
                            for w, x in ((wt1h, Ph), (wt1l, Ph), (wt1h, Pl)):
                                i = pe.matmul(o_, w[:, t, ms], x[:, s, t, :], start=False, stop=t == 1 and x is Pl)
                        i.then_inc(m1_ready, 1)
                if 1 <= s <= blocks:
                    if s == 1:
                        pe.wait_ge(z_read, Z_CREDIT + groups)
                    pe.wait_ge(m1_read, 4 * s)
                    for m in range(H2 // 128):
                        if s >= 2:
                            pe.wait_ge(m2_read, 2 * (s - 2) + m + 1)
                        for t in range(H1 // 128):
                            i = pe.matmul(m2_ps[:, m, :], wt2[:, t, m * 128:(m + 1) * 128], h1[:, (s - 1) % 2, t, :],
                                          start=t == 0, stop=t == H1 // 128 - 1)
                        i.then_inc(m2_ready, 1)
                if s >= 2:
                    pe.wait_ge(m2_read, 2 * (s - 1))
                    if s >= 3:
                        pe.wait_ge(m3_read, s - 2)
                    for t in range(H2 // 128):
                        i = pe.matmul(m3_ps[0:1, :], wt3[:, t:t + 1], h2[:, (s - 2) % 2, t, :],
                                      start=t == 0, stop=t == H2 // 128 - 1)
                    i.then_inc(m3_ready, 1)


def kernel(**inputs):
    import numpy as np
    import concourse.bacc as bacc
    from concourse.bass_utils import run_bass_kernel_spmd

    a = {k: np.ascontiguousarray(v) for k, v in inputs.items()}
    i = np.arange(NF)
    sel0 = np.zeros((2, NF, T0 + 1, NO, NF), np.float32)
    sel0[:, i, T0, 0, i] = 1
    inc = np.zeros((NO, NF, T0, NF), np.float32)
    w = a["L0_rec_w0"]
    w0a = np.zeros((NO, NF, T0, S), w.dtype)
    w0b = np.zeros((NO, NF, T0, S), w.dtype)
    for t in range(T0):
        for r in range(NO):
            offset = NO * t + r
            if offset > NF // 2:
                continue
            j = (i + offset) % NF
            sel0[:, i, t, r, i] = 1
            sel0[:, j, t, r, i] = 1
            w0a[r, :, t] = w[i, j]
            if offset:
                w0b[r, :, t] = w[j, i]
                inc[r, i, t, i] = 1
                inc[r, i, t, j] = 1

    def tiled(w):
        p = w[[field(t, j) for t in range(T1) for j in range(2)]]
        return np.ascontiguousarray(p.reshape(T1, 2 * K1, S).transpose(1, 0, 2))

    def stacked(x):
        p = np.zeros((3, GAP, x.shape[1]), x.dtype)
        p[:, :DENSE] = x
        return p.reshape(DX, -1)

    arrays = {
        "ids": a["ids"],
        "sel0": sel0.reshape(R2, T0 + 1, R0), "inc": inc.reshape(R0, T0, NF),
        "w0a": w0a.reshape(R0, T0, S), "w0b": w0b.reshape(R0, T0, S),
        "w1": tiled(a["L0_rec_w1"]), "w2": tiled(a["L0_rec_w2"]),
        "b": np.ascontiguousarray(np.stack([a["L0_rec_b0"], a["L0_rec_b1"], a["L0_rec_b2"]], axis=1)),
        "dense": stacked(a["dense_ctx"].T),
        "wt1": a["W_top1"], "wx": stacked(a["W_top1"][256:]), "bt1": np.ascontiguousarray(a["b_top1"].reshape(H1 // 128, 128).T),
        "wt2": a["W_top2"], "bt2": np.ascontiguousarray(a["b_top2"].reshape(H2 // 128, 128).T),
        "wt3": np.ascontiguousarray(a["W_top3"].reshape(H2 // 128, 128).T),
    }
    names = list(arrays)
    for f in range(NF):
        arrays[f"tbl_{f}"] = a[f"tbl_{f}"]
    nc = bacc.Bacc("TRN2", target_bir_lowering=False, num_devices=1)
    ap = {k: nc.dram_tensor(f"{k}_in", v.shape, mybir.dt.from_np(v.dtype), kind="ExternalInput").ap()
          for k, v in arrays.items()}
    out = nc.dram_tensor("y_out", (BATCH, 1), F32, kind="ExternalOutput").ap()
    x0_dram = nc.dram_tensor("x0_dram", (SCRATCH, NF, N), F32, kind="Internal").ap()
    build(nc, ap["ids"], [ap[f"tbl_{f}"] for f in range(NF)], x0_dram, *[ap[k] for k in names[1:]], out)
    return run_bass_kernel_spmd(nc, [{f"{k}_in": v for k, v in arrays.items()}], core_ids=[0]).results[0]["y_out"]
```
